# Optimizing a Trainium2 kernel written in Bass

```python
import numpy as np
import jax
import jax.numpy as jnp

def _softmax(x, axis=-1):
    return jax.nn.softmax(x, axis=axis)

def _gelu(x):
    return jax.nn.gelu(x, approximate=True)

def _silu(x):
    return jax.nn.silu(x)

def _sigmoid(x):
    return jax.nn.sigmoid(x)

def _layernorm(x, axis=-1, eps=1e-05):
    m = jnp.mean(x, axis=axis, keepdims=True)
    v = jnp.var(x, axis=axis, keepdims=True)
    return (x - m) / jnp.sqrt(v + eps)

def _scatter_add(tgt, idx, src, axis=0):
    return tgt.at[idx].add(src)

def _segment_sum(src, seg, n):
    return jax.ops.segment_sum(src, seg, n)
kernel_name = 'mk_xattn_seq_d2_seqx_r8_a37470'

def setup_inputs(seed: int=0):
    np.random.seed(seed)
    _w = jnp.asarray

    def _rec_inputs():
        import jax
        import jax.numpy as jnp
        _rk = jax.random.key(seed)
        x = -0.000125 + 0.9999 * jax.random.normal(jax.random.fold_in(_rk, 1), (32, 56, 256), jnp.float32)
        _lenS = 56 - jax.random.randint(jax.random.fold_in(_rk, 7), (32,), 0, max(1, 56 // 4) + 1, jnp.int32)
        _lenS2 = 1500 - jax.random.randint(jax.random.fold_in(_rk, 8), (32,), 0, max(1, 1500 // 4) + 1, jnp.int32)
        _ctx_1024P = jax.random.normal(jax.random.fold_in(_rk, 11), (32, 16, 128), jnp.float32)
        _ctx_1024c = jax.random.dirichlet(jax.random.fold_in(_rk, 511), 0.3 * jnp.ones((16,), jnp.float32), (32, 1500))
        _ctx_1024t = jnp.einsum('bsk,bkd->bsd', _ctx_1024c, _ctx_1024P)
        _ctx_1024t = _ctx_1024t * jax.lax.rsqrt(jnp.mean(jnp.square(_ctx_1024t)) + 1e-12) * 0.953939
        ctx_1024 = 4.13588e-05 + 0.999923 * (_ctx_1024t + 0.3 * jax.random.normal(jax.random.fold_in(_rk, 611), (32, 1500, 128), jnp.float32))
        _validS = jnp.arange(56)[None, :] < _lenS[:, None]
        _validS2 = jnp.arange(1500)[None, :] < _lenS2[:, None]
        _causal = jnp.tril(jnp.ones((56, 56), dtype=bool))
        mask_BxS2_bk0 = jnp.logical_not(jnp.broadcast_to(_validS2[:, :], (32, 1500)))
        return (x, ctx_1024, mask_BxS2_bk0)
    x, ctx_1024, mask_BxS2_bk0 = _rec_inputs()

    def _L0_xattn_setup():
        import jax, jax.numpy as jnp
        import numpy as np
        EPS = 1e-06

        def _rmsnorm(x, w):
            var = jnp.mean(jnp.square(x), axis=-1, keepdims=True)
            return x * jax.lax.rsqrt(var + EPS) * w
        key = jax.random.key(seed)
        ks = jax.random.split(key, 6)
        B, N, M = (4, 512, 256)
        d_model, memory_dim = (256, 128)
        hidden_states = jax.random.normal(ks[0], (B, N, d_model), dtype=jnp.float32)
        memory = jax.random.normal(ks[1], (B, M, memory_dim), dtype=jnp.float32)
        W_mem = jax.random.normal(ks[2], (d_model, memory_dim), dtype=jnp.float32) / np.sqrt(memory_dim)
        W_gate = jax.random.normal(ks[3], (d_model, 2 * d_model), dtype=jnp.float32) / np.sqrt(2 * d_model)
        b_gate = jax.random.normal(ks[4], (d_model,), dtype=jnp.float32) * 0.01
        norm_w = jnp.ones((d_model,), dtype=jnp.float32)
        return {'hidden_states': hidden_states, 'memory': memory, 'W_mem': W_mem, 'W_gate': W_gate, 'b_gate': b_gate, 'norm_w': norm_w}
    _L0_xattn_all = _L0_xattn_setup()
    _L0_xattn_in = {k: v for k, v in _L0_xattn_all.items() if k in ('W_mem', 'W_gate', 'b_gate', 'norm_w')}
    del _L0_xattn_all

    def _L1_xattn_setup():
        import jax, jax.numpy as jnp
        import numpy as np
        DIM = 256
        DIM_MEDIA = 128
        HEADS = 16
        DIM_HEAD = 64
        INNER = HEADS * DIM_HEAD
        FF_INNER = 4 * DIM
        B, N_TOK, N_LAT = (4, 256, 64)
        EPS = 1e-05

        def layernorm(x, g, b):
            mu = jnp.mean(x, axis=-1, keepdims=True)
            var = jnp.var(x, axis=-1, keepdims=True)
            return (x - mu) * jax.lax.rsqrt(var + EPS) * g + b
        key = jax.random.key(seed)
        ks = jax.random.split(key, 12)
        x = jax.random.normal(ks[0], (B, N_TOK, DIM), dtype=jnp.float32)
        media = jax.random.normal(ks[1], (B, N_LAT, DIM_MEDIA), dtype=jnp.float32)
        media_mask = jax.random.randint(ks[2], (B, N_LAT), 0, 2).astype(bool)
        media_mask = media_mask.at[:, 0].set(True)
        s = lambda d: 1.0 / np.sqrt(d)
        Wq = jax.random.normal(ks[3], (DIM, INNER), dtype=jnp.float32) * s(DIM)
        Wkv = jax.random.normal(ks[4], (DIM_MEDIA, 2 * INNER), dtype=jnp.float32) * s(DIM_MEDIA)
        Wo = jax.random.normal(ks[5], (INNER, DIM), dtype=jnp.float32) * s(INNER)
        W1 = jax.random.normal(ks[6], (DIM, FF_INNER), dtype=jnp.float32) * s(DIM)
        W2 = jax.random.normal(ks[7], (FF_INNER, DIM), dtype=jnp.float32) * s(FF_INNER)
        return {'x': x, 'media': media, 'media_mask': media_mask, 'ln_q_g': jnp.ones((DIM,), jnp.float32), 'ln_q_b': jnp.zeros((DIM,), jnp.float32), 'Wq': Wq, 'Wkv': Wkv, 'Wo': Wo, 'attn_gate': jax.random.normal(ks[8], (1,), jnp.float32) * 0.5, 'ln_ff_g': jnp.ones((DIM,), jnp.float32), 'ln_ff_b': jnp.zeros((DIM,), jnp.float32), 'W1': W1, 'W2': W2, 'ff_gate': jax.random.normal(ks[9], (1,), jnp.float32) * 0.5}
    _L1_xattn_all = _L1_xattn_setup()
    _L1_xattn_in = {k: v for k, v in _L1_xattn_all.items() if k in ('ln_q_g', 'ln_q_b', 'Wq', 'Wkv', 'Wo', 'attn_gate', 'ln_ff_g', 'ln_ff_b', 'W1', 'W2', 'ff_gate')}
    del _L1_xattn_all
    return {'x': x, 'ctx_1024': ctx_1024, 'mask_BxS2_bk0': mask_BxS2_bk0, 'L0_xattn_W_mem': _L0_xattn_in['W_mem'], 'L0_xattn_W_gate': _L0_xattn_in['W_gate'], 'L0_xattn_b_gate': _L0_xattn_in['b_gate'], 'L0_xattn_norm_w': _L0_xattn_in['norm_w'], 'L1_xattn_ln_q_g': _L1_xattn_in['ln_q_g'], 'L1_xattn_ln_q_b': _L1_xattn_in['ln_q_b'], 'L1_xattn_Wq': _L1_xattn_in['Wq'], 'L1_xattn_Wkv': _L1_xattn_in['Wkv'], 'L1_xattn_Wo': _L1_xattn_in['Wo'], 'L1_xattn_attn_gate': _L1_xattn_in['attn_gate'], 'L1_xattn_ln_ff_g': _L1_xattn_in['ln_ff_g'], 'L1_xattn_ln_ff_b': _L1_xattn_in['ln_ff_b'], 'L1_xattn_W1': _L1_xattn_in['W1'], 'L1_xattn_W2': _L1_xattn_in['W2'], 'L1_xattn_ff_gate': _L1_xattn_in['ff_gate']}

def reference(x, ctx_1024, mask_BxS2_bk0, L0_xattn_W_mem, L0_xattn_W_gate, L0_xattn_b_gate, L0_xattn_norm_w, L1_xattn_ln_q_g, L1_xattn_ln_q_b, L1_xattn_Wq, L1_xattn_Wkv, L1_xattn_Wo, L1_xattn_attn_gate, L1_xattn_ln_ff_g, L1_xattn_ln_ff_b, L1_xattn_W1, L1_xattn_W2, L1_xattn_ff_gate):
    import jax
    import jax.numpy as jnp

    def _L0_xattn_ref(hidden_states, memory, W_mem, W_gate, b_gate, norm_w):
        import jax, jax.numpy as jnp
        import numpy as np
        EPS = 1e-06

        def _rmsnorm(x, w):
            var = jnp.mean(jnp.square(x), axis=-1, keepdims=True)
            return x * jax.lax.rsqrt(var + EPS) * w
        D = hidden_states.shape[-1]
        memory_proj = jnp.einsum('bme,de->bmd', memory, W_mem)
        scores = jnp.einsum('bnd,bmd->bnm', hidden_states, memory_proj) / jnp.sqrt(jnp.float32(D))
        attn = jax.nn.softmax(scores, axis=-1)
        memory_context = jnp.einsum('bnm,bmd->bnd', attn, memory_proj)
        gate_input = jnp.concatenate([hidden_states, memory_context], axis=-1)
        gate = jax.nn.sigmoid(jnp.einsum('bnf,df->bnd', gate_input, W_gate) + b_gate)
        fused = hidden_states + gate * memory_context
        return _rmsnorm(fused, norm_w)

    def _L1_xattn_ref(x, media, media_mask, ln_q_g, ln_q_b, Wq, Wkv, Wo, attn_gate, ln_ff_g, ln_ff_b, W1, W2, ff_gate):
        import jax, jax.numpy as jnp
        import numpy as np
        DIM = 256
        DIM_MEDIA = 128
        HEADS = 16
        DIM_HEAD = 64
        INNER = HEADS * DIM_HEAD
        FF_INNER = 4 * DIM
        B, N_TOK, N_LAT = (4, 256, 64)
        EPS = 1e-05

        def layernorm(x, g, b):
            mu = jnp.mean(x, axis=-1, keepdims=True)
            var = jnp.var(x, axis=-1, keepdims=True)
            return (x - mu) * jax.lax.rsqrt(var + EPS) * g + b
        scale = DIM_HEAD ** (-0.5)
        qn = layernorm(x, ln_q_g, ln_q_b)
        q = qn @ Wq * scale
        kv = media @ Wkv
        k, v = jnp.split(kv, 2, axis=-1)
        split_heads = lambda t: t.reshape(t.shape[0], t.shape[1], HEADS, DIM_HEAD).transpose(0, 2, 1, 3)
        q, k, v = (split_heads(q), split_heads(k), split_heads(v))
        sim = jnp.einsum('bhid,bhjd->bhij', q, k)
        neg_inf = jnp.finfo(sim.dtype).min
        sim = jnp.where(media_mask[:, None, None, :], sim, neg_inf)
        attn = jax.nn.softmax(sim, axis=-1)
        out = jnp.einsum('bhij,bhjd->bhid', attn, v)
        out = out.transpose(0, 2, 1, 3).reshape(x.shape[0], x.shape[1], INNER)
        attn_out = out @ Wo
        x = x + jnp.tanh(attn_gate) * attn_out
        h = layernorm(x, ln_ff_g, ln_ff_b)
        h = jax.nn.gelu(h @ W1, approximate=False) @ W2
        x = x + jnp.tanh(ff_gate) * h
        return x
    x = _L0_xattn_ref(x, ctx_1024, L0_xattn_W_mem, L0_xattn_W_gate, L0_xattn_b_gate, L0_xattn_norm_w)
    x = _L1_xattn_ref(x, ctx_1024, mask_BxS2_bk0, L1_xattn_ln_q_g, L1_xattn_ln_q_b, L1_xattn_Wq, L1_xattn_Wkv, L1_xattn_Wo, L1_xattn_attn_gate, L1_xattn_ln_ff_g, L1_xattn_ln_ff_b, L1_xattn_W1, L1_xattn_W2, L1_xattn_ff_gate)
    return x

_drawn_inputs = setup_inputs


def setup_inputs(seed=0):
    import zlib

    import numpy as np

    out = dict(_drawn_inputs(seed))
    spreads = {'L0_xattn_norm_w': (1.0, 0.2),
     'L1_xattn_ln_q_g': (1.0, 0.6),
     'L1_xattn_ln_q_b': (0.0, 0.8),
     'L1_xattn_ln_ff_g': (1.0, 0.6),
     'L1_xattn_ln_ff_b': (0.0, 0.8)}
    factors = {'L0_xattn_b_gate': 51.194, 'L1_xattn_W1': 2.735}
    for name, (base, spread) in spreads.items():
        noise = np.random.default_rng([zlib.crc32(name.encode()), seed]).standard_normal(out[name].shape)
        drawn = base * np.exp(spread * noise) if base else spread * noise
        out[name] = jnp.asarray(drawn.astype(out[name].dtype))
    for name, factor in factors.items():
        out[name] = (out[name] * factor).astype(out[name].dtype)
    return out
```

```python
import concourse.bass as bass
from concourse import mybir
from contextlib import ExitStack


def xattn_kernel(nc, x, ctx_in, mask, w_mem, w_gate, b_gate, norm_w, ln_q_g, ln_q_b, wq, wkv, wo,
                 attn_gate, ln_ff_g, ln_ff_b, w1, w2, ff_gate, out):
    fp32, u8, i32 = mybir.dt.float32, mybir.dt.uint8, mybir.dt.int32
    ALU, ACT, AX = mybir.AluOpType, mybir.ActivationFunctionType, mybir.AxisListType

    B, S, D = x.shape
    M, E = ctx_in.shape[1:]
    INNER = wq.shape[1]
    DH = 64
    H = INNER // DH
    F = w1.shape[1]
    NB = 4
    BLOCKS = B // NB
    PAIRS = NB // 2
    SP = 64
    TP = NB * SP
    DT = D // 128
    FT = F // 128
    NCH = 4
    CH = M // NCH
    KT = 3
    KP = CH // KT
    NT = NCH * KT
    G = 2 * S
    U = 2 * G
    UPB = H // 4
    UNITS = NB * UPB
    RING = 3
    T4 = NB * S
    NEG = -3.4028234663852886e38
    EPS0, EPS1 = 1e-6, 1e-5
    V_STEPS = 10

    with ExitStack() as stack:
        def sb(name, shape, dt=fp32):
            return stack.enter_context(nc.sbuf_tensor(name, shape, dt))

        def sem(name):
            return stack.enter_context(nc.semaphore(name))

        wqk = sb("wqk", [128, DT, H, E])
        wvo = sb("wvo", [128, H, D])
        w1_sb = sb("w1_sb", [128, DT, F])
        w2_sb = sb("w2_sb", [128, FT, D])
        wmem = sb("wmem", [128, DT, E])
        wgx = sb("wgx", [128, DT, D])
        wmz = sb("wmz", [128, 2, D])
        bgate_bc = sb("bgate_bc", [128, D])
        normw_bc = sb("normw_bc", [128, D])
        lnq_gb = sb("lnq_gb", [128, 2, DT])
        lnf_gb = sb("lnf_gb", [128, 2, DT])
        gates = sb("gates", [128, 4])
        ident = sb("ident", [128, 128])
        neg_half = sb("neg_half", [128, 2])
        zeros = sb("zeros", [1, U])
        flag_row = sb("flag_row", [1, B * NCH], i32)
        ctx = sb("ctx", [KP, NB, NT, E])
        ctxT = sb("ctxT", [128, NB, M])
        xn = sb("xn", [128, PAIRS, D])
        xT = sb("xT", [128, DT, TP])
        q0T = sb("q0T", [128, TP])
        x1 = sb("x1", [128, PAIRS, D])
        ya = sb("ya", [128, PAIRS, D])
        yb = sb("yb", [128, PAIRS, D])
        y_out = sb("y_out", [128, PAIRS, D])
        qT = sb("qT", [128, NB, H, S])
        oT = sb("oT", [128, H, NB, SP])
        scores = sb("scores", [128, RING, 2, 1536])
        pT = sb("pT", [KP, 2, KT, U])
        mask_u8 = sb("mask_u8", [G, NB, M], u8)
        mbias = sb("mbias", [G, 2, M])
        nmax0 = sb("nmax0", [128, PAIRS])
        sum0 = sb("sum0", [128, PAIRS])
        rsum0 = sb("rsum0", [128, PAIRS])
        ssq = sb("ssq", [128, PAIRS])
        vpe = sb("vpe", [128, PAIRS])
        rstd = sb("rstd", [128, PAIRS])
        bst = sb("bst", [128, PAIRS, 6])
        mv = sb("mv", [128, PAIRS, 2])
        cmax = sb("cmax", [G, RING, 2, NCH])
        nmax = sb("nmax", [G, RING, 2])
        sums = sb("sums", [G, RING, 2, NCH])
        tsum = sb("tsum", [G, RING, 2])
        rsum = sb("rsum", [G, RING, 2])
        any_f = sb("any_f", [B, NCH])
        none_f = sb("none_f", [B, 1])
        flags = sb("flags", [B, NCH], i32)
        st_a = scores[:, 0, :, :].rearrange("p a n -> p (a n)")
        st_b = scores[:, 1, :, :].rearrange("p a n -> p (a n)")
        wq_n = st_a[:, 0:DT * INNER].rearrange("p (t n) -> p t n", t=DT)
        wkv_n = st_b[:, 0:2 * INNER]
        wgate_n = scores[:, 2, 0, 0:DT * 2 * D].rearrange("p (t n) -> p t n", t=DT)
        wo_n = oT[:, 0:H // 2, :, :].rearrange("p h b s -> p h (b s)")
        wqT = ctxT[:, 0:2, :].rearrange("p b m -> p (b m)")[:, 0:8 * D].rearrange("p (j n) -> p j n", j=8)
        wkvT = ctxT[:, 2:4, :].rearrange("p b m -> p (b m)")[:, 0:16 * E].rearrange("p (j n) -> p j n", j=16)
        wgcT = scores[:, 2, 1, 0:DT * D].rearrange("p (t n) -> p t n", t=DT)
        mask_rows = mask_u8[0:B, 0, :]
        p0 = scores[:, 0, :, :]
        p0T = scores[:, 1, :, :]
        lnT, c0T = xT, q0T
        h1T = scores[:, 2, :, :].rearrange("p g n -> p (g n)")[:, 0:FT * TP].rearrange(
            "p (f b s) -> p f b s", f=FT, b=NB)

        ps = stack.enter_context(nc.psum_tensor("ps", [128, 8, 512], fp32))
        XT_BANK, Q0_BANK = 6, 7

        wts_in = sem("wts_in")
        mrow_in = sem("mrow_in")
        flag_in = sem("flag_in")
        ctx_in_s = [sem(f"ctx_in{j}") for j in range(NB)]
        x_in = sem("x_in")
        mask_in = sem("mask_in")
        out_st = sem("out_st")
        p_const = sem("p_const")
        p_mask = sem("p_mask")
        p_stat = sem("p_stat")
        p_pad = sem("p_pad")
        p_step = sem("p_step")
        pe_w = sem("pe_w")
        v_w = sem("v_w")
        v_step = sem("v_step")
        a_gate = sem("a_gate")
        v_flag = sem("v_flag")
        pe_ctxT = sem("pe_ctxT")
        v_ctxT = sem("v_ctxT")
        a_ctxT = sem("a_ctxT")
        pe_xT = sem("pe_xT")
        v_xT = sem("v_xT")
        pe_q0 = sem("pe_q0")
        v_q0 = sem("v_q0")
        pe_zx = sem("pe_zx")
        pe_s0 = sem("pe_s0")
        v_max0 = sem("v_max0")
        a_p0 = sem("a_p0")
        pe_p0T = sem("pe_p0T")
        v_p0T = sem("v_p0T")
        a_p0T = sem("a_p0T")
        pe_c0 = sem("pe_c0")
        v_c0 = sem("v_c0")
        pe_mz = sem("pe_mz")
        v_z = sem("v_z")
        a_z = sem("a_z")
        v_stat = sem("v_stat")
        v_x1 = sem("v_x1")
        v_hat = sem("v_hat")
        pe_hatT = sem("pe_hatT")
        v_lnT = sem("v_lnT")
        pe_q = sem("pe_q")
        a_q = sem("a_q")
        v_q = sem("v_q")
        pe_s = sem("pe_s")
        v_s = sem("v_s")
        v_nmax = sem("v_nmax")
        a_exp = sem("a_exp")
        v_prob = sem("v_prob")
        v_s_zero = sem("v_s_zero")
        v_rs = sem("v_rs")
        pe_pT = sem("pe_pT")
        a_pT = sem("a_pT")
        pe_o = sem("pe_o")
        a_o = sem("a_o")
        pe_att = sem("pe_att")
        pe_h = sem("pe_h")
        a_gelu = sem("a_gelu")
        pe_y = sem("pe_y")
        v_out = sem("v_out")

        block = stack.enter_context(nc.Block())

        ctx_v = ctx_in.rearrange("(i j) (c p t) e -> i j p c (t e)", j=NB, c=NCH, t=KT)
        x_v = x.rearrange("(i b) s d -> i b s d", b=NB)
        out_v = out.rearrange("(i b) s d -> i b s d", b=NB)
        mask_v = mask.rearrange("(i b) m -> i (b m)", b=NB)

        def chunk_flags(eng, i, b):
            return [eng.value_load(flag_row[0:1, bass.ds(NB * NCH * i + NCH * b + c, 1)], min_val=0, max_val=1)
                    for c in range(NCH)]

        def wait_apart(eng, sem, value):
            held = eng.compute_val(value)
            eng.wait_ge(flag_in, 16)
            eng.wait_ge(sem, held)

        def row_bc(v, parts):
            return bass.AP(v.tensor, v.offset, [[0, parts], [1, v.shape[0]]])

        def load_ctx(eng, i, j):
            eng.dma_start(ctx[:, j, :, :].rearrange("p (c t) e -> p c (t e)", t=KT),
                          ctx_v[i, j]).then_inc(ctx_in_s[j], 16)

        def load_x(eng, i):
            for b in range(NB):
                eng.dma_start(xn[SP * (b % 2):SP * (b % 2) + S, b // 2, :], x_v[i, b]).then_inc(x_in, 16)

        def load_mask(eng, i):
            src = mask_v[i]
            eng.dma_start(mask_u8[:, :, :].rearrange("p b m -> p (b m)"),
                          bass.AP(src.tensor, src.offset, [[0, G], [1, NB * M]])).then_inc(mask_in, 16)

        @block.sync
        def _(sp):
            sp.dma_start(mask_rows, mask).then_inc(mrow_in, 16)
            load_ctx(sp, 0, 0)
            sp.wait_ge(p_const, 3)
            load_x(sp, 0)
            for j in range(1, NB):
                load_ctx(sp, 0, j)
            sp.wait_ge(v_flag, 1)
            sp.dma_start(flag_row[0:1, :].rearrange("o (b c) -> o b c", c=NCH),
                         flags[:, :]).then_inc(flag_in, 16)
            load_mask(sp, 0)
            sp.sem_inc(out_st, 16)
            with sp.Fori(0, BLOCKS - 1) as i:
                wait_apart(sp, v_x1, i + 1)
                load_x(sp, i + 1)
                wait_apart(sp, p_mask, NB * i + NB)
                load_mask(sp, i + 1)
                for j in range(NB):
                    wait_apart(sp, pe_o, UNITS * i + UPB * (j + 1))
                    load_ctx(sp, i + 1, j)
                wait_apart(sp, v_out, i + 2)
                for b in range(NB):
                    sp.dma_start(out_v[i, b], y_out[SP * (b % 2):SP * (b % 2) + S, b // 2, :]).then_inc(out_st, 16)
            sp.wait_ge(v_out, BLOCKS + 1)
            for b in range(NB):
                sp.dma_start(out_v[BLOCKS - 1, b],
                             y_out[SP * (b % 2):SP * (b % 2) + S, b // 2, :]).then_inc(out_st, 16)
            sp.wait_ge(out_st, 16 + 16 * NB * BLOCKS)

        @block.gpsimd
        def _(pool):
            nc.gpsimd.memset(ident[:, :], 0.0).then_inc(p_step, 1)
            pool.wait_ge(p_step, 1)
            nc.gpsimd.affine_select(out=ident[:, :], in_=ident[:, :], compare_op=ALU.not_equal, fill=1.0, base=0,
                                    pattern=[[-1, 128]], channel_multiplier=1).then_inc(p_const, 1)
            nc.gpsimd.memset(zeros[:, :], 0.0)
            nc.gpsimd.memset(neg_half[:, :], -0.5).then_inc(p_const, 1)
            nc.gpsimd.memset(xn[:, :, :], 0.0).then_inc(p_const, 1)
            pool.wait_ge(v_w, 14)
            nc.gpsimd.memset(oT[:, :, :, :], 0.0).then_inc(p_const, 1)

            def rsqrt(k, done, i, src, mul, eps):
                wait_apart(pool, v_stat, 3 * i + k + 1)
                nc.gpsimd.tensor_scalar(vpe[:, :], src, mul, eps, ALU.mult, ALU.add).then_inc(p_step, 1)
                pool.wait_ge(p_step, 3 * i + k + 2)
                nc.gpsimd.tensor_tensor(rstd[:, :], vpe[:, :], neg_half[:, :], ALU.pow).then_inc(p_stat, 1)

            def mask_bias(b, i):
                if b >= 2:
                    wait_apart(pool, v_nmax, UNITS * i + UPB * (b - 1))
                if b == 0:
                    wait_apart(pool, mask_in, 16 * i + 16)
                nc.gpsimd.tensor_scalar(
                    mbias[:, b % 2, :].rearrange("g (c t p) -> g c t p", c=NCH, t=KT),
                    mask_u8[:, b, :].rearrange("g (c p t) -> g c t p", c=NCH, t=KT),
                    1.0, -NEG, ALU.subtract, ALU.mult).then_inc(p_mask, 1)

            with pool.Fori(0, BLOCKS) as i:
                rsqrt(0, 0, i, ssq[:, :], 1.0 / D, EPS0)
                rsqrt(1, 0, i, mv[:, :, 1], 1.0, EPS1)
                for b in range(NB):
                    mask_bias(b, i)
                wait_apart(pool, pe_o, UNITS * i + UNITS)
                nc.gpsimd.memset(h1T[:, :, :, S:SP], 0.0).then_inc(p_pad, 1)
                rsqrt(2, 0, i, mv[:, :, 1], 1.0, EPS1)

        @block.scalar
        def _(act):
            def load(dst, src, **kw):
                act.dma_start(dst, src, **kw).then_inc(wts_in, 16)

            load(wq_n, wq.rearrange("(t p) n -> p t n", p=128))
            load(wkv_n, wkv)
            load(wgate_n, w_gate.rearrange("(t p) n -> p t n", p=128))
            load(wo_n, wo.rearrange("(j p) n -> p j n", p=128))
            load(wmem[:, :, :], w_mem.rearrange("(t p) n -> p t n", p=128))
            load(w1_sb[:, :, :], w1.rearrange("(t p) n -> p t n", p=128))
            load(w2_sb[:, :, :], w2.rearrange("(t p) n -> p t n", p=128))
            load(bgate_bc[:, :], row_bc(b_gate, 128))
            load(normw_bc[:, :], row_bc(norm_w, 128))
            for k, (t, v) in enumerate([(lnq_gb, ln_q_g), (lnq_gb, ln_q_b), (lnf_gb, ln_ff_g), (lnf_gb, ln_ff_b)]):
                load(t[:, k % 2, :], v.rearrange("(t p) -> p t", p=128), allow_slow_non_contiguous=True)
            load(gates[:, 0:1], row_bc(attn_gate, 128))
            load(gates[:, 1:2], row_bc(ff_gate, 128))
            act.wait_ge(wts_in, 16 * 15)
            nc.scalar.activation(gates[:, 2:4], gates[:, 0:2], ACT.Tanh).then_inc(a_gate, 1)
            act.wait_ge(flag_in, 16)

            def evac_o(u, i):
                b, k = u // UPB, u % UPB
                act.wait_ge(pe_o, UNITS * i + u + 1)
                nc.scalar.activation(oT[:, 4 * k:4 * k + 4, b, 0:S],
                                     ps[:, 6 + u % 2, 0:U].rearrange("p (h s) -> p h s", s=S),
                                     ACT.Copy).then_inc(a_o, 1)

            def exps(u, i, live):
                r = u % RING
                if u % UPB == 0:
                    live[u // UPB] = chunk_flags(nc.scalar, i, u // UPB)
                wait_apart(act, v_nmax, UNITS * i + u + 1)
                for c in range(NCH):
                    with act.If(live[u // UPB][c] != 0):
                        for gg in range(2):
                            v = scores[0:G, r, gg, c * CH:(c + 1) * CH]
                            ins = nc.scalar.activation(v, v, ACT.Exp, bias=nmax[:, r, gg:gg + 1],
                                                       accum_out=sums[:, r, gg, c:c + 1])
                        ins.then_inc(a_exp, 1)
                    with act.Else():
                        if u or c:
                            act.wait_ge(a_exp, NCH * (UNITS * i + u) + c)
                        act.sem_inc(a_exp, 1)

            def evac_pT(u, i, live):
                for c in range(NCH):
                    slot = (u + c) % 2
                    wait_apart(act, pe_pT, NCH * (UNITS * i + u) + c + 1)
                    with act.If(live[u // UPB][c] != 0):
                        src = ps[0:KP, 2 + 2 * slot:4 + 2 * slot, :].rearrange(
                            "p a (z n) -> p (a z) n", z=2)[:, 0:KT, 0:U]
                        nc.scalar.activation(pT[:, slot, :, :], src, ACT.Copy).then_inc(a_pT, 1)
                    with act.Else():
                        if u or c:
                            act.wait_ge(a_pT, NCH * (UNITS * i + u) + c)
                        act.sem_inc(a_pT, 1)

            with act.Fori(0, BLOCKS) as i:
                live = {}
                for j in (1, 3):
                    act.wait_ge(pe_ctxT, NB * i + j + 1)
                    nc.scalar.activation(ctxT[:, j, :].rearrange("p (a n) -> p a n", a=3), ps[:, 3:6, 0:500],
                                         ACT.Copy).then_inc(a_ctxT, 1)
                for p in range(PAIRS):
                    act.wait_ge(v_max0, PAIRS * i + p + 1)
                    nc.scalar.activation(p0[:, p, 0:M].rearrange("p (a n) -> p a n", a=3),
                                         ps[:, 3 * p:3 * p + 3, 0:500], ACT.Exp, bias=nmax0[:, p:p + 1],
                                         accum_out=sum0[:, p:p + 1]).then_inc(a_p0, 1)
                act.wait_ge(pe_p0T, PAIRS * i + 2)
                nc.scalar.activation(p0T[0:KP, 1, :], ps[0:KP, 3:6, :].rearrange("p a n -> p (a n)"),
                                     ACT.Copy).then_inc(a_p0T, 1)
                act.wait_ge(v_z, PAIRS * i + PAIRS)
                nc.scalar.activation(yb[:, :, :], ya[:, :, :], ACT.Exp, scale=-1.0).then_inc(a_z, 1)
                for hp in range(0, H // 2, 2):
                    act.wait_ge(pe_q, 8 * i + hp + 1)
                    nc.scalar.activation(
                        qT[:, :, 2 * hp:2 * hp + 2, :].rearrange("p b h s -> p h b s"),
                        ps[:, hp % 4, 0:2 * T4].rearrange("p (h b s) -> p h b s", h=2, s=S),
                        ACT.Copy).then_inc(a_q, 1)
                exps(0, i, live)
                exps(1, i, live)
                for u in range(UNITS):
                    evac_pT(u, i, live)
                    if u + 2 < UNITS:
                        exps(u + 2, i, live)
                    evac_o(u, i)
                for k in range(FT // 2):
                    act.wait_ge(pe_h, 4 * i + k + 1)
                    nc.scalar.activation(h1T[:, 2 * k:2 * k + 2, :, 0:S],
                                         ps[:, 2 + k, 0:2 * T4].rearrange("p (f b s) -> p f b s", f=2, s=S),
                                         ACT.Gelu).then_inc(a_gelu, 1)

        @block.vector
        def _(dve):
            dve.wait_ge(mrow_in, 16)
            nc.vector.tensor_reduce(any_f[:, :], mask_rows.rearrange("b (c n) -> b c n", c=NCH), AX.X,
                                    ALU.max).then_inc(v_step, 1)
            dve.wait_ge(v_step, 1)
            nc.vector.tensor_reduce(none_f[:, :], any_f[:, :], AX.X, ALU.max).then_inc(v_step, 1)
            dve.wait_ge(v_step, 2)
            nc.vector.tensor_scalar(none_f[:, :], none_f[:, :], -1.0, 1.0, ALU.mult, ALU.add).then_inc(v_step, 1)
            dve.wait_ge(v_step, 3)
            nc.vector.tensor_scalar(flags[:, :], any_f[:, :], none_f[:, 0:1], None, ALU.max).then_inc(v_flag, 1)

            def emptied(n):
                dve.wait_ge(pe_w, n)

            for t in range(2):
                for k in range(2):
                    emptied(2 * t + k + 1)
                    nc.vector.tensor_copy(wqT[:, 4 * k:4 * k + 4, t * 128:(t + 1) * 128],
                                          ps[:, 2 * t + k, :].rearrange("p (j n) -> p j n", j=4)).then_inc(v_w, 1)
            for k in range(4):
                emptied(5 + k)
                nc.vector.tensor_copy(wkvT[:, 4 * k:4 * k + 4, :],
                                      ps[:, 4 + k, :].rearrange("p (j n) -> p j n", j=4)).then_inc(v_w, 1)
            emptied(9)
            nc.vector.tensor_copy(wgx[:, :, :], ps[:, 0, :].rearrange("p (t n) -> p t n", t=DT)).then_inc(v_w, 1)
            emptied(10)
            nc.vector.tensor_copy(wgcT, ps[:, 1, :].rearrange("p (t n) -> p t n", t=DT)).then_inc(v_w, 1)
            emptied(11)
            nc.vector.tensor_copy(wmz[:, 0, :], ps[:, 2, 0:D]).then_inc(v_w, 1)
            emptied(12)
            nc.vector.tensor_copy(wmz[:, 1, :], ps[:, 3, 0:D]).then_inc(v_w, 1)
            dve.wait_ge(a_gate, 1)
            for k in range(2):
                emptied(13 + k)
                nc.vector.tensor_scalar(
                    wvo[:, k::2, :], ps[:, 4 * k:4 * k + 4, :].rearrange("p a (z n) -> p (a z) n", z=2),
                    gates[:, 2:3], None, ALU.mult).then_inc(v_w, 1)
            for k in range(4):
                emptied(15 + k)
                for par in range(2):
                    h0 = 4 * k + par
                    ins = nc.vector.tensor_scalar(
                        wqk[:, :, h0:h0 + 3:2, :],
                        ps[:, 2 * k + par, :].rearrange("p (t h n) -> p t h n", t=DT, h=2),
                        0.125, None, ALU.mult)
                ins.then_inc(v_w, 1)
            nc.vector.tensor_scalar(w2_sb[:, :, :], w2_sb[:, :, :], gates[:, 3:4], None,
                                    ALU.mult).then_inc(v_w, 1)
            dve.wait_ge(flag_in, 16)
            dve.wait_ge(p_const, 4)

            def scores_in(u, i, live):
                r, b = u % RING, u // UPB
                if u % UPB == 0:
                    live[b] = chunk_flags(nc.vector, i, b)
                    wait_apart(dve, p_mask, NB * i + b + 1)
                n = 2 * NCH * (UNITS * i + u)
                for c in range(NCH):
                    with dve.If(live[b][c] != 0):
                        for gg in range(2):
                            wait_apart(dve, pe_s, n + 2 * c + gg + 1)
                            nc.vector.tensor_tensor_reduce(
                                out=scores[0:G, r, gg, c * CH:(c + 1) * CH], in0=ps[0:G, gg, 0:CH],
                                in1=mbias[:, b % 2, c * CH:(c + 1) * CH], scale=1.0, scalar=NEG,
                                op0=ALU.add, op1=ALU.max,
                                accum_out=cmax[:, r, gg, c:c + 1]).then_inc(v_s, 1)
                    with dve.Else():
                        nc.vector.memset(cmax[:, r, :, c:c + 1], NEG).then_inc(v_s, 2)
                nc.vector.memset(sums[:, r, :, :], 0.0).then_inc(v_s_zero, 1)
                dve.wait_ge(v_s, n + 2 * NCH)
                dve.wait_ge(v_s_zero, UNITS * i + u + 1)
                nc.vector.tensor_reduce(nmax[:, r, :], cmax[:, r, :, :], AX.X, ALU.max,
                                        negate=True).then_inc(v_nmax, 1)

            def normalise(u, i, live):
                r, b = u % RING, u // UPB
                n = NCH * (UNITS * i + u)
                dve.wait_ge(a_exp, n + NCH)
                nc.vector.tensor_reduce(tsum[:, r, :], sums[:, r, :, :], AX.X, ALU.add).then_inc(v_rs, 1)
                dve.wait_ge(v_rs, 2 * (UNITS * i + u) + 1)
                nc.vector.reciprocal(rsum[:, r, :], tsum[:, r, :]).then_inc(v_rs, 1)
                wait_apart(dve, v_rs, 2 * (UNITS * i + u) + 2)
                for c in range(NCH):
                    with dve.If(live[b][c] != 0):
                        for gg in range(2):
                            v = scores[0:G, r, gg, c * CH:(c + 1) * CH]
                            ins = nc.vector.tensor_scalar(v, v, rsum[:, r, gg:gg + 1], None, ALU.mult)
                        ins.then_inc(v_prob, 1)
                    with dve.Else():
                        if u or c:
                            dve.wait_ge(v_prob, n + c)
                        dve.sem_inc(v_prob, 1)

            dve.sem_inc(v_out, 1)
            with dve.Fori(0, BLOCKS) as i:
                live = {}
                steps = [0]

                def step(ins, apart=False):
                    steps[0] += 1
                    ins.then_inc(v_step, 1)
                    (wait_apart if apart else type(dve).wait_ge)(dve, v_step, V_STEPS * i + (3 + steps[0]))

                for j in (0, 2):
                    dve.wait_ge(pe_ctxT, NB * i + j + 1)
                    nc.vector.tensor_copy(ctxT[:, j, :].rearrange("p (a n) -> p a n", a=3),
                                          ps[:, 0:3, 0:500]).then_inc(v_ctxT, 1)
                dve.wait_ge(pe_xT, i + 1)
                nc.vector.tensor_copy(xT[:, :, :].rearrange("p t n -> p (t n)"), ps[:, XT_BANK, :]).then_inc(v_xT, 1)
                dve.wait_ge(pe_q0, i + 1)
                nc.vector.tensor_scalar(q0T[:, :], ps[:, Q0_BANK, 0:TP], float(D) ** -0.5, None,
                                        ALU.mult).then_inc(v_q0, 1)
                dve.wait_ge(pe_zx, i + 1)
                for p in range(PAIRS):
                    step(nc.vector.tensor_tensor(ya[:, p, :], ps[:, XT_BANK, p * D:(p + 1) * D], bgate_bc[:, :],
                                                 ALU.add))
                for p in range(PAIRS):
                    dve.wait_ge(pe_s0, PAIRS * i + p + 1)
                    nc.vector.tensor_reduce(nmax0[:, p:p + 1], ps[:, 3 * p:3 * p + 3, 0:500], AX.XY, ALU.max,
                                            negate=True).then_inc(v_max0, 1)
                dve.wait_ge(pe_p0T, PAIRS * i + 1)
                nc.vector.tensor_copy(p0T[0:KP, 0, :], ps[0:KP, 0:3, :].rearrange("p a n -> p (a n)")).then_inc(v_p0T, 1)
                dve.wait_ge(a_p0, PAIRS * i + PAIRS)
                step(nc.vector.reciprocal(rsum0[:, :], sum0[:, :]))
                dve.wait_ge(pe_c0, i + 1)
                nc.vector.tensor_copy(c0T[:, :], ps[:, Q0_BANK, 0:TP]).then_inc(v_c0, 1)
                for p in range(PAIRS):
                    dve.wait_ge(pe_mz, PAIRS * i + p + 1)
                    nc.vector.scalar_tensor_tensor(out=ya[:, p, :], in0=ps[:, 3 * p, D:2 * D],
                                                   scalar=rsum0[:, p:p + 1], in1=ya[:, p, :],
                                                   op0=ALU.mult, op1=ALU.add).then_inc(v_z, 1)
                dve.wait_ge(a_z, i + 1)
                step(nc.vector.tensor_scalar(yb[:, :, :], yb[:, :, :], 1.0, None, ALU.add))
                step(nc.vector.reciprocal(yb[:, :, :], yb[:, :, :]))
                for p in range(PAIRS):
                    ins = nc.vector.scalar_tensor_tensor(out=yb[:, p, :], in0=ps[:, 3 * p, 0:D],
                                                         scalar=rsum0[:, p:p + 1], in1=yb[:, p, :],
                                                         op0=ALU.mult, op1=ALU.mult)
                step(ins)
                step(nc.vector.tensor_tensor(yb[:, :, :], yb[:, :, :], xn[:, :, :], ALU.add))
                for p in range(PAIRS):
                    ins = nc.vector.tensor_tensor_reduce(out=ya[:, p, :], in0=yb[:, p, :], in1=yb[:, p, :],
                                                         scale=1.0, scalar=0.0, op0=ALU.mult, op1=ALU.add,
                                                         accum_out=ssq[:, p:p + 1])
                ins.then_inc(v_stat, 1)
                dve.wait_ge(p_stat, 3 * i + 1)
                for p in range(PAIRS):
                    ins = nc.vector.scalar_tensor_tensor(out=x1[:, p, :], in0=yb[:, p, :], scalar=rstd[:, p:p + 1],
                                                         in1=normw_bc[:, :], op0=ALU.mult, op1=ALU.mult)
                ins.then_inc(v_x1, 1)
                dve.wait_ge(v_x1, i + 1)

                def layernorm(src, k):
                    for p in range(PAIRS):
                        ins = nc.vector.bn_stats(bst[:, p, :], src[:, p, :])
                    step(ins, apart=True)
                    for p in range(PAIRS):
                        ins = nc.vector.bn_aggr(mv[:, p, :], bst[:, p, :])
                    ins.then_inc(v_stat, 1)
                    dve.wait_ge(v_stat, 3 * i + k + 1)
                    dve.wait_ge(p_stat, 3 * i + k + 1)
                    for p in range(PAIRS):
                        ins = nc.vector.tensor_scalar(yb[:, p, :], src[:, p, :], mv[:, p, 0:1], rstd[:, p:p + 1],
                                                      ALU.subtract, ALU.mult)
                    ins.then_inc(v_hat, 1)

                def scale_shift(gb, k):
                    dve.wait_ge(pe_hatT, 2 * i + k)
                    for t in range(DT):
                        ins = nc.vector.tensor_scalar(lnT[:, t, :], ps[:, XT_BANK, t * TP:(t + 1) * TP],
                                                      gb[:, 0, t:t + 1], gb[:, 1, t:t + 1], ALU.mult, ALU.add)
                    ins.then_inc(v_lnT, 1)

                layernorm(x1, 1)
                scale_shift(lnq_gb, 1)
                for hp in range(1, H // 2, 2):
                    dve.wait_ge(pe_q, 8 * i + hp + 1)
                    nc.vector.tensor_copy(
                        qT[:, :, 2 * hp:2 * hp + 2, :].rearrange("p b h s -> p h b s"),
                        ps[:, hp % 4, 0:2 * T4].rearrange("p (h b s) -> p h b s", h=2, s=S)).then_inc(v_q, 1)
                scores_in(0, i, live)
                scores_in(1, i, live)
                for u in range(UNITS):
                    normalise(u, i, live)
                    if u + 2 < UNITS:
                        scores_in(u + 2, i, live)
                for p in range(PAIRS):
                    dve.wait_ge(pe_att, PAIRS * i + p + 1)
                    ins = nc.vector.tensor_tensor(x1[:, p, :], ps[:, p, 0:D], x1[:, p, :], ALU.add)
                step(ins)
                layernorm(x1, 2)
                scale_shift(lnf_gb, 2)
                dve.wait_ge(out_st, 16 * NB * i + 16)
                for p in range(PAIRS):
                    dve.wait_ge(pe_y, PAIRS * i + p + 1)
                    ins = nc.vector.tensor_tensor(y_out[:, p, :], ps[:, 6 + p, 0:D], x1[:, p, :], ALU.add)
                ins.then_inc(v_out, 1)
                assert steps[0] == V_STEPS, steps[0]

        @block.tensor
        def _(pe):
            mm, tr = nc.tensor.matmul, nc.tensor.transpose
            pe.wait_ge(p_const, 1)
            pe.wait_ge(wts_in, 16 * 15)
            for t in range(2):
                for k in range(2):
                    for j in range(4):
                        c = 4 * k + j
                        ins = tr(ps[:, 2 * t + k, j * 128:(j + 1) * 128], wq_n[:, t, c * 128:(c + 1) * 128], ident[:, :])
                    ins.then_inc(pe_w, 1)
            for k in range(4):
                for j in range(4):
                    c = 4 * k + j
                    ins = tr(ps[:, 4 + k, j * 128:(j + 1) * 128], wkv_n[:, c * 128:(c + 1) * 128], ident[:, :])
                ins.then_inc(pe_w, 1)
            for half in range(2):
                pe.wait_ge(v_w, half + 1)
                for f in range(DT):
                    for o in range(DT):
                        c = DT * half + f
                        ins = tr(ps[:, half, f * D + o * 128:f * D + (o + 1) * 128],
                                 wgate_n[:, o, c * 128:(c + 1) * 128], ident[:, :])
                ins.then_inc(pe_w, 1)
            pe.wait_ge(v_w, 3)
            for t in range(DT):
                ins = tr(ps[:, 2, t * 128:(t + 1) * 128], wmem[:, t, :], ident[:, :])
            ins.then_inc(pe_w, 1)
            pe.wait_ge(v_w, 10)
            for t in range(DT):
                ins = mm(ps[:, 3, 0:D], wmem[:, t, :], wgcT[:, t, :], start=(t == 0), stop=(t == DT - 1))
            ins.then_inc(pe_w, 1)
            pe.wait_ge(v_w, 12)
            for par in range(2):
                for j in range(H // 2):
                    rows = slice(64 * par, 64 * par + 64)
                    ins = mm(ps[:, 4 * par + j // 2, (j % 2) * D:(j % 2 + 1) * D], wkvT[rows, 8 + j, :],
                             wo_n[rows, j, :], start=True, stop=True)
                ins.then_inc(pe_w, 1)
            for k in range(4):
                pe.wait_ge(v_w, 13 + k // 2)
                for par in range(2):
                    rows = slice(64 * par, 64 * par + 64)
                    for t in range(DT):
                        for jj in range(2):
                            j = 2 * k + jj
                            c0 = (2 * t + jj) * E
                            ins = mm(ps[:, 2 * k + par, c0:c0 + E], wqT[rows, j, t * 128:(t + 1) * 128],
                                     wkvT[rows, j, :], start=True, stop=True)
                ins.then_inc(pe_w, 1)
            pe.wait_ge(flag_in, 16)
            pe.wait_ge(v_w, 19)
            pe.wait_ge(p_const, 4)

            def layer1_scores(u, i, live):
                b, k = u // UPB, u % UPB
                n = 2 * NCH * (UNITS * i + u)
                if k == 0:
                    live[b] = chunk_flags(nc.tensor, i, b)
                for c in range(NCH):
                    with pe.If(live[b][c] != 0):
                        for gg in range(2):
                            if u or c:
                                pe.wait_ge(v_s, n + 2 * c - 1 + gg)
                            h0 = 4 * k + 2 * gg
                            mm(ps[0:G, gg, 0:CH], qT[:, b, h0:h0 + 2, :].rearrange("p h s -> p (h s)"),
                               ctxT[:, b, c * CH:(c + 1) * CH], start=True, stop=True).then_inc(pe_s, 1)
                    with pe.Else():
                        if u or c:
                            pe.wait_ge(pe_s, n + 2 * c)
                        pe.sem_inc(pe_s, 2)

            def layer1_pT(u, i, live):
                b, r = u // UPB, u % RING
                n = NCH * (UNITS * i + u)
                for c in range(NCH):
                    slot = (u + c) % 2
                    with pe.If(live[b][c] != 0):
                        pe.wait_ge(v_prob, n + c + 1)
                        if c == 1 and u:
                            pe.wait_ge(a_pT, n - 1)
                        elif c != 1 and (u or c):
                            pe.wait_ge(a_pT, n + max(c - 1, 0))
                        for t in range(KT):
                            for gg in range(2):
                                col = (t % 2) * 256 + gg * G
                                ins = tr(ps[0:KP, 2 + 2 * slot + t // 2, col:col + G],
                                         scores[0:G, r, gg, c * CH + t * KP:c * CH + (t + 1) * KP], ident[0:G, 0:G])
                        ins.then_inc(pe_pT, 1)
                    with pe.Else():
                        if u or c:
                            pe.wait_ge(pe_pT, n + c)
                        pe.sem_inc(pe_pT, 1)
                    layer1_pv(u, c, i, live) if c < NCH - 1 else None

            def layer1_pv(u, c, i, live):
                b, slot = u // UPB, (u + c) % 2
                if c == 0:
                    if u >= 2:
                        pe.wait_ge(a_o, UNITS * i + u - 1)
                    mm(ps[:, 6 + u % 2, 0:U], ctx[0:1, b, 0, :], zeros[0:1, :], start=True, stop=False,
                       skip_group_check=True)
                with pe.If(live[b][c] != 0):
                    pe.wait_ge(a_pT, NCH * (UNITS * i + u) + c + 1)
                    for t in range(KT):
                        mm(ps[:, 6 + u % 2, 0:U], ctx[:, b, KT * c + t, :], pT[:, slot, t, :],
                           start=False, stop=False, skip_group_check=True)

            def layer1_close(u, i):
                mm(ps[:, 6 + u % 2, 0:U], ctx[0:1, u // UPB, 0, :], zeros[0:1, :], start=False, stop=True,
                   skip_group_check=True).then_inc(pe_o, 1)

            with pe.Fori(0, BLOCKS) as i:
                live = {}
                for j in range(NB):
                    pe.wait_ge(ctx_in_s[j], 16 * i + 16)
                    if j == 2:
                        pe.wait_ge(v_ctxT, 2 * i + 1)
                    if j == 3:
                        pe.wait_ge(a_ctxT, 2 * i + 1)
                    for t in range(NT):
                        ins = tr(ps[:, 3 * (j % 2) + t // 4, (t % 4) * KP:(t % 4 + 1) * KP], ctx[:, j, t, :],
                                 ident[0:KP, 0:KP])
                    ins.then_inc(pe_ctxT, 1)
                pe.wait_ge(x_in, 16 * NB * i + 16 * NB)
                pe.wait_ge(v_out, i + 1)
                for t in range(DT):
                    for p in range(PAIRS):
                        ins = tr(ps[:, XT_BANK, t * TP + p * 128:t * TP + (p + 1) * 128],
                                 xn[:, p, t * 128:(t + 1) * 128], ident[:, :])
                ins.then_inc(pe_xT, 1)
                pe.wait_ge(v_xT, i + 1)
                for t in range(DT):
                    ins = mm(ps[:, Q0_BANK, 0:TP], wmem[:, t, :], xT[:, t, :], start=(t == 0), stop=(t == DT - 1))
                ins.then_inc(pe_q0, 1)
                for p in range(PAIRS):
                    for t in range(DT):
                        ins = mm(ps[:, XT_BANK, p * D:(p + 1) * D], xT[:, t, p * 128:(p + 1) * 128], wgx[:, t, :],
                                 start=(t == 0), stop=(t == DT - 1))
                ins.then_inc(pe_zx, 1)
                pe.wait_ge(v_q0, i + 1)
                pe.wait_ge(v_ctxT, 2 * i + 2)
                pe.wait_ge(a_ctxT, 2 * i + 2)
                for p in range(PAIRS):
                    for k in range(3):
                        for hb in range(2):
                            j = 2 * p + hb
                            ins = mm(ps[SP * hb:SP * hb + SP, 3 * p + k, 0:500], q0T[:, j * SP:(j + 1) * SP],
                                     ctxT[:, j, k * 500:(k + 1) * 500], start=True, stop=True)
                    ins.then_inc(pe_s0, 1)
                for p in range(PAIRS):
                    pe.wait_ge(a_p0, PAIRS * i + p + 1)
                    for t in range(NT):
                        ins = tr(ps[0:KP, 3 * p + t // 4, (t % 4) * 128:(t % 4 + 1) * 128],
                                 p0[:, p, t * KP:(t + 1) * KP], ident[:, :])
                    ins.then_inc(pe_p0T, 1)
                for p in range(PAIRS):
                    pe.wait_ge(v_p0T if p == 0 else a_p0T, i + 1)
                    for hb in range(2):
                        j = 2 * p + hb
                        for t in range(NT):
                            ins = mm(ps[:, Q0_BANK, j * SP:(j + 1) * SP], ctx[:, j, t, :],
                                     p0T[0:KP, p, t * 128 + hb * SP:t * 128 + hb * SP + SP],
                                     start=(t == 0), stop=(t == NT - 1))
                ins.then_inc(pe_c0, 1)
                pe.wait_ge(v_c0, i + 1)
                for p in range(PAIRS):
                    mm(ps[:, 3 * p, :], c0T[:, p * 128:(p + 1) * 128],
                       wmz[:, :, :].rearrange("p a n -> p (a n)"), start=True, stop=True).then_inc(pe_mz, 1)

                def hat_transposes(k):
                    pe.wait_ge(v_hat, 2 * i + k)
                    for t in range(DT):
                        for p in range(PAIRS):
                            ins = tr(ps[:, XT_BANK, t * TP + p * 128:t * TP + (p + 1) * 128],
                                     yb[:, p, t * 128:(t + 1) * 128], ident[:, :])
                    ins.then_inc(pe_hatT, 1)
                    pe.wait_ge(v_lnT, 2 * i + k)

                hat_transposes(1)
                tok = [lnT[:, t, :].rearrange("p (b s) -> p b s", s=SP)[:, :, 0:S] for t in range(DT)]
                for hp in range(H // 2):
                    if hp >= 4:
                        pe.wait_ge((a_q, v_q)[hp % 2], 4 * i + (hp - 4) // 2 + 1)
                    for h in range(2):
                        for t in range(DT):
                            ins = mm(ps[:, hp % 4, h * T4:(h + 1) * T4], wqk[:, t, 2 * hp + h, :], tok[t],
                                     start=(t == 0), stop=(t == DT - 1))
                    ins.then_inc(pe_q, 1)
                pe.wait_ge(a_q, 4 * i + 4)
                pe.wait_ge(v_q, 4 * i + 4)
                layer1_scores(0, i, live)
                layer1_scores(1, i, live)
                for u in range(UNITS):
                    layer1_pT(u, i, live)
                    if u + 2 < UNITS:
                        layer1_scores(u + 2, i, live)
                    layer1_pv(u, NCH - 1, i, live)
                    layer1_close(u, i)
                pe.wait_ge(a_o, UNITS * i + UNITS)
                for p in range(PAIRS):
                    for h in range(H):
                        ins = mm(ps[:, p, 0:D], oT[:, h, 2 * p:2 * p + 2, :].rearrange("p b s -> p (b s)"),
                                 wvo[:, h, :], start=(h == 0), stop=(h == H - 1))
                    ins.then_inc(pe_att, 1)
                hat_transposes(2)
                for k in range(FT // 2):
                    for f in range(2):
                        for t in range(DT):
                            ft = 2 * k + f
                            ins = mm(ps[:, 2 + k, f * T4:(f + 1) * T4], w1_sb[:, t, ft * 128:(ft + 1) * 128], tok[t],
                                     start=(t == 0), stop=(t == DT - 1))
                    ins.then_inc(pe_h, 1)
                pe.wait_ge(a_gelu, 4 * i + 4)
                pe.wait_ge(p_pad, i + 1)
                for p in range(PAIRS):
                    for f in range(FT):
                        ins = mm(ps[:, 6 + p, 0:D], h1T[:, f, 2 * p:2 * p + 2, :].rearrange("p b s -> p (b s)"),
                                 w2_sb[:, f, :], start=(f == 0), stop=(f == FT - 1))
                    ins.then_inc(pe_y, 1)


_INS = ['x', 'ctx_1024', 'mask_BxS2_bk0', 'L0_xattn_W_mem', 'L0_xattn_W_gate', 'L0_xattn_b_gate',
        'L0_xattn_norm_w', 'L1_xattn_ln_q_g', 'L1_xattn_ln_q_b', 'L1_xattn_Wq', 'L1_xattn_Wkv', 'L1_xattn_Wo',
        'L1_xattn_attn_gate', 'L1_xattn_ln_ff_g', 'L1_xattn_ln_ff_b', 'L1_xattn_W1', 'L1_xattn_W2',
        'L1_xattn_ff_gate']


def kernel(**inputs):
    import numpy as _np
    import concourse.bacc as _bacc
    from concourse import mybir as _mybir
    from concourse.bass_utils import run_bass_kernel_spmd as _run

    nc = _bacc.Bacc("TRN2", target_bir_lowering=False, num_devices=1)
    arrays, args = {}, []
    for name in _INS:
        a = _np.ascontiguousarray(inputs[name])
        arrays[f"in_{name}_dram"] = a
        args.append(nc.dram_tensor(f"in_{name}_dram", a.shape, _mybir.dt.from_np(a.dtype), kind="ExternalInput").ap())
    shape = inputs['x'].shape
    args.append(nc.dram_tensor("out_0_dram", shape, _mybir.dt.float32, kind="ExternalOutput").ap())
    xattn_kernel(nc, *args)
    r = _run(nc, [arrays], core_ids=[0])
    return r.results[0]["out_0_dram"]
```

```python
import concourse.bass as bass
from concourse import mybir
from contextlib import ExitStack


def xattn_kernel(nc, x, ctx_in, mask, w_mem, w_gate, b_gate, norm_w, ln_q_g, ln_q_b, wq, wkv, wo,
                 attn_gate, ln_ff_g, ln_ff_b, w1, w2, ff_gate, out):
    fp32, u8, i32 = mybir.dt.float32, mybir.dt.uint8, mybir.dt.int32
    ALU, ACT, AX = mybir.AluOpType, mybir.ActivationFunctionType, mybir.AxisListType

    B, S, D = x.shape
    M, E = ctx_in.shape[1:]
    INNER = wq.shape[1]
    DH = 64
    H = INNER // DH
    F = w1.shape[1]
    NB = 4
    BLOCKS = B // NB
    PAIRS = NB // 2
    SP = 64
    TP = NB * SP
    DT = D // 128
    FT = F // 128
    NCH = 4
    CH = M // NCH
    LAST = M - CH
    KT = 3
    KP = CH // KT
    NT = NCH * KT
    G = 2 * S
    U = 2 * G
    UPB = H // 4
    UNITS = NB * UPB
    RING = 3
    T4 = NB * S
    NEG = -3.4028234663852886e38
    EPS0, EPS1 = 1e-6, 1e-5
    A_STEPS, D_STEPS = 8, 1
    PS, VS = 2 * NCH, 2 * NCH + 2

    with ExitStack() as stack:
        def sb(name, shape, dt=fp32):
            return stack.enter_context(nc.sbuf_tensor(name, shape, dt))

        def sem(name):
            return stack.enter_context(nc.semaphore(name))

        wqk = sb("wqk", [128, DT, H, E])
        wvo = sb("wvo", [128, H, D])
        w1_sb = sb("w1_sb", [128, DT, F])
        w2_sb = sb("w2_sb", [128, FT, D])
        wmem = sb("wmem", [128, DT, E])
        wgx = sb("wgx", [128, DT, D])
        wmz = sb("wmz", [128, 2, D])
        bgate_bc = sb("bgate_bc", [128, D])
        normw_bc = sb("normw_bc", [128, D])
        lnq_gb = sb("lnq_gb", [128, 2, DT])
        lnf_gb = sb("lnf_gb", [128, 2, DT])
        gates = sb("gates", [128, 4])
        ident = sb("ident", [128, 128])
        neg_half = sb("neg_half", [128, 2])
        zeros = sb("zeros", [1, 128])
        flag_row = sb("flag_row", [1, B * NCH], i32)
        slow_row = sb("slow_row", [1, BLOCKS], i32)
        ctx = sb("ctx", [KP, NB, NT, E])
        ctxT = sb("ctxT", [128, NB, M])
        xn = sb("xn", [128, PAIRS, D])
        xT = sb("xT", [128, DT, TP])
        q0T = sb("q0T", [128, TP])
        x1 = sb("x1", [128, PAIRS, D])
        x2 = sb("x2", [128, PAIRS, D])
        ffT = sb("ffT", [128, DT, TP])
        ya = sb("ya", [128, PAIRS, D])
        yb = sb("yb", [128, PAIRS, D])
        qT = sb("qT", [128, NB, H, S])
        oT = sb("oT", [128, H, NB, SP])
        scores = sb("scores", [128, RING, 2, 1536])
        pT = sb("pT", [KP, 2, KT, U])
        mask_u8 = sb("mask_u8", [G, 2, M], u8)
        mbias = sb("mbias", [G, 2, M])
        nmax0 = sb("nmax0", [128, PAIRS])
        sum0 = sb("sum0", [128, PAIRS])
        rsum0 = sb("rsum0", [128, PAIRS])
        ssq = sb("ssq", [128, PAIRS])
        vpe = [sb(f"vpe{k}", [128, PAIRS]) for k in range(2)]
        rstd = [sb(f"rstd{k}", [128, PAIRS]) for k in range(2)]
        bst = [sb(f"bst{k}", [128, PAIRS, 6]) for k in range(2)]
        mv = [sb(f"mv{k}", [128, PAIRS, 2]) for k in range(2)]
        cmin = sb("cmin", [G, RING, 2, NCH])
        nmax = sb("nmax", [G, RING, 2])
        sums = sb("sums", [G, RING, 2, NCH])
        tsum = sb("tsum", [G, RING, 2])
        rsum = sb("rsum", [G, RING, 2])
        any_f = sb("any_f", [B, NCH])
        none_f = sb("none_f", [B, 1])
        flags = sb("flags", [B, NCH], i32)
        st_a = scores[:, 0, :, :].rearrange("p a n -> p (a n)")
        st_b = scores[:, 1, :, :].rearrange("p a n -> p (a n)")
        wq_n = st_a[:, 0:DT * INNER].rearrange("p (t n) -> p t n", t=DT)
        wkv_n = st_b[:, 0:2 * INNER]
        wgate_n = scores[:, 2, 0, 0:DT * 2 * D].rearrange("p (t n) -> p t n", t=DT)
        wo_n = oT[:, 0:H // 2, :, :].rearrange("p h b s -> p h (b s)")
        wqT = ctxT[:, 0:2, :].rearrange("p b m -> p (b m)")[:, 0:8 * D].rearrange("p (j n) -> p j n", j=8)
        wkvT = ctxT[:, 2:4, :].rearrange("p b m -> p (b m)")[:, 0:16 * E].rearrange("p (j n) -> p j n", j=16)
        wgcT = scores[:, 2, 1, 0:DT * D].rearrange("p (t n) -> p t n", t=DT)
        mask_rows = mask_u8[0:B, 0, :]
        yd = sb("yd", [128, PAIRS, D])
        p0 = scores[:, 0, :, :]
        p0T = scores[:, 1, :, :]
        lnT, c0T = xT, q0T
        h1T = scores[:, 2, :, :].rearrange("p g n -> p (g n)")[:, 0:FT * TP].rearrange(
            "p (f b s) -> p f b s", f=FT, b=NB)

        ps = stack.enter_context(nc.psum_tensor("ps", [128, 8, 512], fp32))
        SET = (2, 5)
        ATT, HATD, W1B, C0B, YB = (0, 1), 0, (1, 0), 1, (0, 1)
        XTB, Q0B, ZXB, HATA, QB = 2, 3, 4, 3, (4, 5, 6, 7)

        wts_in = sem("wts_in")
        mrow_in = sem("mrow_in")
        flag_in = sem("flag_in")
        ctx_in_s = [sem(f"ctx_in{j}") for j in range(NB)]
        x_in = sem("x_in")
        mask_in = [sem(f"mask_in{k}") for k in range(2)]
        out_st = sem("out_st")
        p_const = sem("p_const")
        p_mask = sem("p_mask")
        p_stat = sem("p_stat")
        p_pad = sem("p_pad")
        p_step = sem("p_step")
        pe_w = sem("pe_w")
        v_w = sem("v_w")
        v_step = sem("v_step")
        v_stepd = sem("v_stepd")
        a_gate = sem("a_gate")
        v_flag = sem("v_flag")
        pe_ctxT = sem("pe_ctxT")
        v_ctxT = sem("v_ctxT")
        a_ctxT = sem("a_ctxT")
        pe_xT = sem("pe_xT")
        v_xT = sem("v_xT")
        pe_q0 = sem("pe_q0")
        v_q0 = sem("v_q0")
        pe_zx = sem("pe_zx")
        pe_s0 = sem("pe_s0")
        v_max0 = sem("v_max0")
        a_p0 = sem("a_p0")
        pe_p0T = sem("pe_p0T")
        v_p0T = sem("v_p0T")
        a_p0T = sem("a_p0T")
        pe_c0 = sem("pe_c0")
        v_c0 = sem("v_c0")
        pe_mz = sem("pe_mz")
        v_z = sem("v_z")
        a_z = sem("a_z")
        v_slow = sem("v_slow")
        v_stat = sem("v_stat")
        v_statd = sem("v_statd")
        p_statd = sem("p_statd")
        p_stepd = sem("p_stepd")
        v_x2 = sem("v_x2")
        v_hatd = sem("v_hatd")
        pe_hatdT = sem("pe_hatdT")
        v_ffT = sem("v_ffT")
        v_x1 = sem("v_x1")
        v_hat = sem("v_hat")
        pe_hatT = sem("pe_hatT")
        v_lnT = sem("v_lnT")
        pe_q = sem("pe_q")
        a_q = sem("a_q")
        v_q = sem("v_q")
        pe_s = sem("pe_s")
        v_s = sem("v_s")
        a_exp = sem("a_exp")
        v_prob = sem("v_prob")
        v_rs = sem("v_rs")
        pe_pT = sem("pe_pT")
        a_pT = sem("a_pT")
        pe_o = sem("pe_o")
        a_o = sem("a_o")
        pe_att = sem("pe_att")
        pe_h = sem("pe_h")
        a_gelu = sem("a_gelu")
        pe_y = sem("pe_y")
        v_out = sem("v_out")

        block = stack.enter_context(nc.Block())

        ctx_v = ctx_in.rearrange("(i j) (c p t) e -> i j p c (t e)", j=NB, c=NCH, t=KT)
        x_v = x.rearrange("(i b) s d -> i b s d", b=NB)
        out_v = out.rearrange("(i b) s d -> i b s d", b=NB)
        mask_v = mask.rearrange("(i b) m -> i b m", b=NB)

        def chunk_flags(eng, i, b):
            return [eng.value_load(flag_row[0:1, bass.ds(NB * NCH * i + NCH * b + c, 1)], min_val=0, max_val=1)
                    for c in range(NCH)]

        def wait_apart(eng, sem, value):
            held = eng.compute_val(value)
            eng.wait_ge(flag_in, 16)
            eng.wait_ge(sem, held)

        def is_slow(eng, i):
            return eng.value_load(slow_row[0:1, bass.ds(i, 1)], min_val=0, max_val=1)

        def row_bc(v, parts):
            return bass.AP(v.tensor, v.offset, [[0, parts], [1, v.shape[0]]])

        def load_ctx(eng, i, j):
            eng.dma_start(ctx[:, j, :, :].rearrange("p (c t) e -> p c (t e)", t=KT),
                          ctx_v[i, j]).then_inc(ctx_in_s[j], 16)

        def load_x(eng, i):
            for b in range(NB):
                eng.dma_start(xn[SP * (b % 2):SP * (b % 2) + S, b // 2, :], x_v[i, b]).then_inc(x_in, 16)

        def load_mask(eng, i, b):
            eng.dma_start(mask_u8[:, b % 2, :], bass.AP(mask_v.tensor, mask_v[i, b].offset, [[0, G], [1, M]])
                          ).then_inc(mask_in[b % 2], 16)

        @block.sync
        def _(sp):
            sp.dma_start(mask_rows, mask).then_inc(mrow_in, 16)
            load_ctx(sp, 0, 0)
            sp.wait_ge(p_const, 3)
            load_x(sp, 0)
            for j in range(1, NB):
                load_ctx(sp, 0, j)
            sp.wait_ge(v_flag, 1)
            sp.dma_start(flag_row[0:1, :].rearrange("o (b c) -> o b c", c=NCH),
                         flags[:, :]).then_inc(flag_in, 16)
            load_mask(sp, 0, 0)
            load_mask(sp, 0, 1)

            def store(i):
                for b in range(NB):
                    sp.dma_start(out_v[i, b], yd[SP * (b % 2):SP * (b % 2) + S, b // 2, :]).then_inc(out_st, 16)

            sp.sem_inc(out_st, 16)
            with sp.Fori(0, BLOCKS - 1) as i:
                for b in (2, 3):
                    wait_apart(sp, p_mask, NB * i + b - 1)
                    load_mask(sp, i, b)
                wait_apart(sp, v_x1, i + 1)
                load_x(sp, i + 1)
                for j in range(NB):
                    wait_apart(sp, pe_o, UNITS * i + UPB * (j + 1))
                    load_ctx(sp, i + 1, j)
                for b in (0, 1):
                    wait_apart(sp, p_mask, NB * i + b + 3)
                    load_mask(sp, i + 1, b)
                wait_apart(sp, v_out, i + 2)
                store(i)
            last = BLOCKS - 1
            for b in (2, 3):
                sp.wait_ge(p_mask, NB * last + b - 1)
                load_mask(sp, last, b)
            sp.wait_ge(v_out, BLOCKS + 1)
            store(last)
            sp.wait_ge(out_st, 16 + 16 * NB * BLOCKS)

        @block.gpsimd
        def _(pool):
            nc.gpsimd.memset(ident[:, :], 0.0).then_inc(p_step, 1)
            pool.wait_ge(p_step, 1)
            nc.gpsimd.affine_select(out=ident[:, :], in_=ident[:, :], compare_op=ALU.not_equal, fill=1.0, base=0,
                                    pattern=[[-1, 128]], channel_multiplier=1).then_inc(p_const, 1)
            nc.gpsimd.memset(zeros[:, :], 0.0)
            nc.gpsimd.memset(neg_half[:, :], -0.5).then_inc(p_const, 1)
            nc.gpsimd.memset(xn[:, :, :], 0.0).then_inc(p_const, 1)
            pool.wait_ge(v_w, 14)
            nc.gpsimd.memset(oT[:, :, :, :], 0.0).then_inc(p_const, 1)

            pool.wait_ge(flag_in, 16)

            def rsqrt(src, mul, eps, stage, stat, n, own, done, m):
                wait_apart(pool, stat, n)
                nc.gpsimd.tensor_scalar(vpe[stage][:, :], src, mul, eps, ALU.mult, ALU.add).then_inc(own, 1)
                wait_apart(pool, own, m)
                nc.gpsimd.tensor_tensor(rstd[stage][:, :], vpe[stage][:, :], neg_half[:, :], ALU.pow).then_inc(done, 1)

            def front_stats(i):
                rsqrt(ssq[:, :], 1.0 / D, EPS0, 0, v_stat, 2 * i + 1, p_step, p_stat, 2 * i + 2)
                rsqrt(mv[0][:, :, 1], 1.0, EPS1, 0, v_stat, 2 * i + 2, p_step, p_stat, 2 * i + 3)

            def tail_stats(i):
                rsqrt(mv[1][:, :, 1], 1.0, EPS1, 1, v_statd, i + 1, p_stepd, p_statd, i + 1)

            def mask_bias(i, b):
                if b >= 2:
                    wait_apart(pool, v_s, VS * (UNITS * i + UPB * (b - 1)))
                wait_apart(pool, mask_in[b % 2], 32 * i + 16 * (b // 2) + 16)
                nc.gpsimd.tensor_scalar(
                    mbias[:, b % 2, :].rearrange("g (c t p) -> g c t p", c=NCH, t=KT),
                    mask_u8[:, b % 2, :].rearrange("g (c p t) -> g c t p", c=NCH, t=KT),
                    1.0, -NEG, ALU.subtract, ALU.mult).then_inc(p_mask, 1)

            mask_bias(0, 0)
            mask_bias(0, 1)
            front_stats(0)
            with pool.Fori(0, BLOCKS - 1) as i:
                mask_bias(i, 2)
                mask_bias(i, 3)
                wait_apart(pool, pe_o, UNITS * i + UNITS)
                nc.gpsimd.memset(h1T[:, :, :, S:SP], 0.0).then_inc(p_pad, 1)
                tail_stats(i)
                mask_bias(i + 1, 0)
                mask_bias(i + 1, 1)
                front_stats(i + 1)
            mask_bias(BLOCKS - 1, 2)
            mask_bias(BLOCKS - 1, 3)
            pool.wait_ge(pe_o, UNITS * BLOCKS)
            nc.gpsimd.memset(h1T[:, :, :, S:SP], 0.0).then_inc(p_pad, 1)
            tail_stats(BLOCKS - 1)

        @block.scalar
        def _(act):
            def load(dst, src, **kw):
                act.dma_start(dst, src, **kw).then_inc(wts_in, 16)

            load(wq_n, wq.rearrange("(t p) n -> p t n", p=128))
            load(wkv_n, wkv)
            load(wgate_n, w_gate.rearrange("(t p) n -> p t n", p=128))
            load(wo_n, wo.rearrange("(j p) n -> p j n", p=128))
            load(wmem[:, :, :], w_mem.rearrange("(t p) n -> p t n", p=128))
            load(w1_sb[:, :, :], w1.rearrange("(t p) n -> p t n", p=128))
            load(w2_sb[:, :, :], w2.rearrange("(t p) n -> p t n", p=128))
            load(bgate_bc[:, :], row_bc(b_gate, 128))
            load(normw_bc[:, :], row_bc(norm_w, 128))
            for k, (t, v) in enumerate([(lnq_gb, ln_q_g), (lnq_gb, ln_q_b), (lnf_gb, ln_ff_g), (lnf_gb, ln_ff_b)]):
                load(t[:, k % 2, :], v.rearrange("(t p) -> p t", p=128), allow_slow_non_contiguous=True)
            load(gates[:, 0:1], row_bc(attn_gate, 128))
            load(gates[:, 1:2], row_bc(ff_gate, 128))
            act.wait_ge(wts_in, 16 * 15)
            nc.scalar.activation(gates[:, 2:4], gates[:, 0:2], ACT.Tanh).then_inc(a_gate, 1)
            act.wait_ge(flag_in, 16)
            act.wait_ge(v_slow, 1)

            def evac_o(u, i):
                b, k = u // UPB, u % UPB
                act.wait_ge(pe_o, UNITS * i + u + 1)
                nc.scalar.activation(oT[:, 4 * k:4 * k + 4, b, 0:S],
                                     ps[:, 6 + u % 2, 0:U].rearrange("p (h s) -> p h s", s=S),
                                     ACT.Copy).then_inc(a_o, 1)

            def exp_chunk(u, c):
                r = u % RING
                for gg in range(2):
                    v = scores[0:G, r, gg, c * CH:(c + 1) * CH]
                    ins = nc.scalar.activation(v, v, ACT.Exp, bias=nmax[:, r, gg:gg + 1], scale=-1.0,
                                               accum_out=sums[:, r, gg, c:c + 1])
                return ins

            def exps(u, i, live):
                if u % UPB == 0:
                    live[u // UPB] = chunk_flags(nc.scalar, i, u // UPB)
                wait_apart(act, v_s, VS * (UNITS * i + u + 1))
                for c in range(NCH):
                    with act.If(live[u // UPB][c] != 0):
                        exp_chunk(u, c).then_inc(a_exp, 1)
                    with act.Else():
                        if u or c:
                            act.wait_ge(a_exp, NCH * (UNITS * i + u) + c)
                        act.sem_inc(a_exp, 1)

            def copy_pT(u, c):
                slot = (u + c) % 2
                src = ps[0:KP, 2 + 2 * slot:4 + 2 * slot, :].rearrange("p a (z n) -> p (a z) n", z=2)[:, 0:KT, 0:U]
                return nc.scalar.activation(pT[:, slot, :, :], src, ACT.Copy)

            def evac_pT(u, i, live):
                for c in range(NCH):
                    slot = (u + c) % 2
                    wait_apart(act, pe_pT, NCH * (UNITS * i + u) + c + 1)
                    with act.If(live[u // UPB][c] != 0):
                        copy_pT(u, c).then_inc(a_pT, 1)
                    with act.Else():
                        if u or c:
                            act.wait_ge(a_pT, NCH * (UNITS * i + u) + c)
                        act.sem_inc(a_pT, 1)

            def attention_all(i):
                live = {}
                exps(0, i, live)
                exps(1, i, live)
                for u in range(UNITS):
                    evac_pT(u, i, live)
                    if u + 2 < UNITS:
                        exps(u + 2, i, live)
                    evac_o(u, i)

            def exps_last(u, i):
                r = u % RING
                act.wait_ge(v_s, VS * (UNITS * i + u + 1))
                for gg in range(2):
                    v = scores[0:G, r, gg, LAST:M]
                    ins = nc.scalar.activation(v, v, ACT.Exp, bias=cmin[:, r, gg, NCH - 1:NCH], scale=-1.0,
                                               accum_out=sums[:, r, gg, NCH - 1:NCH])
                ins.then_inc(a_exp, NCH)

            def attention_last(i):
                exps_last(0, i)
                exps_last(1, i)
                for u in range(UNITS):
                    act.wait_ge(pe_pT, NCH * (UNITS * i + u + 1))
                    copy_pT(u, NCH - 1).then_inc(a_pT, NCH)
                    if u + 2 < UNITS:
                        exps_last(u + 2, i)
                    evac_o(u, i)

            def attention(i):
                slow = is_slow(nc.scalar, i)
                with act.If(slow != 0):
                    attention_all(i)
                with act.Else():
                    attention_last(i)

            def context_in(i, j):
                act.wait_ge(pe_ctxT, NB * i + j + 1)
                nc.scalar.activation(ctxT[:, j, :].rearrange("p (a n) -> p a n", a=3),
                                     ps[:, SET[1]:SET[1] + 3, 0:500], ACT.Copy).then_inc(a_ctxT, 1)

            def front(i):
                for p in range(PAIRS):
                    act.wait_ge(v_max0, PAIRS * i + p + 1)
                    nc.scalar.activation(p0[:, p, 0:M].rearrange("p (a n) -> p a n", a=3),
                                         ps[:, SET[p]:SET[p] + 3, 0:500], ACT.Exp, bias=nmax0[:, p:p + 1],
                                         accum_out=sum0[:, p:p + 1]).then_inc(a_p0, 1)
                act.wait_ge(pe_p0T, PAIRS * i + 2)
                nc.scalar.activation(p0T[0:KP, 1, :], ps[0:KP, SET[1]:SET[1] + 3, :].rearrange("p a n -> p (a n)"),
                                     ACT.Copy).then_inc(a_p0T, 1)
                act.wait_ge(v_z, PAIRS * i + PAIRS)
                nc.scalar.activation(yb[:, :, :], ya[:, :, :], ACT.Exp, scale=-1.0).then_inc(a_z, 1)

            def queries_in(i):
                for hp in range(0, H // 2, 2):
                    act.wait_ge(pe_q, 8 * i + hp + 1)
                    nc.scalar.activation(
                        qT[:, :, 2 * hp:2 * hp + 2, :].rearrange("p b h s -> p h b s"),
                        ps[:, QB[hp % 4], 0:2 * T4].rearrange("p (h b s) -> p h b s", h=2, s=S),
                        ACT.Copy).then_inc(a_q, 1)

            def gelus(i):
                for k in range(FT // 2):
                    act.wait_ge(pe_h, 4 * i + k + 1)
                    nc.scalar.activation(h1T[:, 2 * k:2 * k + 2, :, 0:S],
                                         ps[:, W1B[k % 2], 0:2 * T4].rearrange("p (f b s) -> p f b s", f=2, s=S),
                                         ACT.Gelu).then_inc(a_gelu, 1)

            context_in(0, 1)
            context_in(0, 3)
            front(0)
            queries_in(0)
            with act.Fori(0, BLOCKS - 1) as i:
                attention(i)
                context_in(i + 1, 1)
                context_in(i + 1, 3)
                gelus(i)
                front(i + 1)
                queries_in(i + 1)
            attention(BLOCKS - 1)
            gelus(BLOCKS - 1)

        @block.vector
        def _(dve):
            dve.wait_ge(mrow_in, 16)
            nc.vector.tensor_reduce(any_f[:, :], mask_rows.rearrange("b (c n) -> b c n", c=NCH), AX.X,
                                    ALU.max).then_inc(v_step, 1)
            dve.wait_ge(v_step, 1)
            nc.vector.tensor_reduce(none_f[:, :], any_f[:, :], AX.X, ALU.max).then_inc(v_step, 1)
            dve.wait_ge(v_step, 2)
            nc.vector.tensor_scalar(none_f[:, :], none_f[:, :], -1.0, 1.0, ALU.mult, ALU.add).then_inc(v_step, 1)
            dve.wait_ge(v_step, 3)
            nc.vector.tensor_scalar(flags[:, :], any_f[:, :], none_f[:, 0:1], None, ALU.max).then_inc(v_flag, 1)

            def emptied(n):
                dve.wait_ge(pe_w, n)

            for t in range(2):
                for k in range(2):
                    emptied(2 * t + k + 1)
                    nc.vector.tensor_copy(wqT[:, 4 * k:4 * k + 4, t * 128:(t + 1) * 128],
                                          ps[:, 2 * t + k, :].rearrange("p (j n) -> p j n", j=4)).then_inc(v_w, 1)
            for k in range(4):
                emptied(5 + k)
                nc.vector.tensor_copy(wkvT[:, 4 * k:4 * k + 4, :],
                                      ps[:, 4 + k, :].rearrange("p (j n) -> p j n", j=4)).then_inc(v_w, 1)
            emptied(9)
            nc.vector.tensor_copy(wgx[:, :, :], ps[:, 0, :].rearrange("p (t n) -> p t n", t=DT)).then_inc(v_w, 1)
            emptied(10)
            nc.vector.tensor_copy(wgcT, ps[:, 1, :].rearrange("p (t n) -> p t n", t=DT)).then_inc(v_w, 1)
            emptied(11)
            nc.vector.tensor_copy(wmz[:, 0, :], ps[:, 2, 0:D]).then_inc(v_w, 1)
            emptied(12)
            nc.vector.tensor_copy(wmz[:, 1, :], ps[:, 3, 0:D]).then_inc(v_w, 1)
            dve.wait_ge(a_gate, 1)
            for k in range(2):
                emptied(13 + k)
                nc.vector.tensor_scalar(
                    wvo[:, k::2, :], ps[:, 4 * k:4 * k + 4, :].rearrange("p a (z n) -> p (a z) n", z=2),
                    gates[:, 2:3], None, ALU.mult).then_inc(v_w, 1)
            for k in range(4):
                emptied(15 + k)
                for par in range(2):
                    h0 = 4 * k + par
                    ins = nc.vector.tensor_scalar(
                        wqk[:, :, h0:h0 + 3:2, :],
                        ps[:, 2 * k + par, :].rearrange("p (t h n) -> p t h n", t=DT, h=2),
                        0.125, None, ALU.mult)
                ins.then_inc(v_w, 1)
            nc.vector.tensor_scalar(w2_sb[:, :, :], w2_sb[:, :, :], gates[:, 3:4], None,
                                    ALU.mult).then_inc(v_w, 1)
            dve.wait_ge(flag_in, 16)
            nc.vector.tensor_reduce(slow_row[:, :], flag_row[0:1, :].rearrange(
                "o (i b c) -> o i b c", b=NB, c=NCH)[:, :, :, 0:NCH - 1], AX.XY, ALU.max).then_inc(v_slow, 1)
            dve.wait_ge(v_slow, 1)
            dve.wait_ge(p_const, 4)

            def add_mask(u, c):
                r, b = u % RING, u // UPB
                return [lambda gg=gg: nc.vector.tensor_tensor_reduce(
                    out=scores[0:G, r, gg, c * CH:(c + 1) * CH], in0=ps[0:G, gg, 0:CH],
                    in1=mbias[:, b % 2, c * CH:(c + 1) * CH], scale=-1.0, scalar=-NEG,
                    op0=ALU.add, op1=ALU.min, accum_out=cmin[:, r, gg, c:c + 1]) for gg in range(2)]

            def scale_probs(u, c):
                r = u % RING
                for gg in range(2):
                    v = scores[0:G, r, gg, c * CH:(c + 1) * CH]
                    ins = nc.vector.tensor_scalar(v, v, rsum[:, r, gg:gg + 1], None, ALU.mult)
                return ins

            def scores_in(u, i, live):
                r, b = u % RING, u // UPB
                if u % UPB == 0:
                    live[b] = chunk_flags(nc.vector, i, b)
                    wait_apart(dve, p_mask, NB * i + b + 1)
                n, m = PS * (UNITS * i + u), VS * (UNITS * i + u)
                for c in range(NCH):
                    with dve.If(live[b][c] != 0):
                        for gg, add in enumerate(add_mask(u, c)):
                            wait_apart(dve, pe_s, n + 2 * c + gg + 1)
                            add().then_inc(v_s, 1)
                    with dve.Else():
                        nc.vector.memset(cmin[:, r, :, c:c + 1], -NEG).then_inc(v_s, 2)
                nc.vector.memset(sums[:, r, :, :], 0.0).then_inc(v_s, 1)
                dve.wait_ge(v_s, m + VS - 1)
                nc.vector.tensor_reduce(nmax[:, r, :], cmin[:, r, :, :], AX.X, ALU.min).then_inc(v_s, 1)

            def normalise(u, i, live):
                r, b = u % RING, u // UPB
                n = NCH * (UNITS * i + u)
                dve.wait_ge(a_exp, n + NCH)
                nc.vector.tensor_reduce(tsum[:, r, :], sums[:, r, :, :], AX.X, ALU.add).then_inc(v_rs, 1)
                dve.wait_ge(v_rs, 2 * (UNITS * i + u) + 1)
                nc.vector.reciprocal(rsum[:, r, :], tsum[:, r, :]).then_inc(v_rs, 1)
                wait_apart(dve, v_rs, 2 * (UNITS * i + u) + 2)
                for c in range(NCH):
                    with dve.If(live[b][c] != 0):
                        scale_probs(u, c).then_inc(v_prob, 1)
                    with dve.Else():
                        if u or c:
                            dve.wait_ge(v_prob, n + c)
                        dve.sem_inc(v_prob, 1)

            def attention_all(i):
                live = {}
                scores_in(0, i, live)
                scores_in(1, i, live)
                normalise(0, i, live)
                for u in range(UNITS):
                    if u + 1 < UNITS:
                        normalise(u + 1, i, live)
                    if u + 2 < UNITS:
                        scores_in(u + 2, i, live)

            def scores_last(u, i):
                if u % UPB == 0:
                    dve.wait_ge(p_mask, NB * i + u // UPB + 1)
                for gg, add in enumerate(add_mask(u, NCH - 1)):
                    wait_apart(dve, pe_s, PS * (UNITS * i + u) + PS // 2 * (gg + 1))
                    add().then_inc(v_s, VS // 2)

            def normalise_last(u, i):
                r = u % RING
                dve.wait_ge(a_exp, NCH * (UNITS * i + u + 1))
                nc.vector.reciprocal(rsum[:, r, :], sums[:, r, :, NCH - 1]).then_inc(v_rs, 2)
                dve.wait_ge(v_rs, 2 * (UNITS * i + u + 1))
                scale_probs(u, NCH - 1).then_inc(v_prob, NCH)

            def attention_last(i):
                scores_last(0, i)
                scores_last(1, i)
                normalise_last(0, i)
                for u in range(UNITS):
                    if u + 1 < UNITS:
                        normalise_last(u + 1, i)
                    if u + 2 < UNITS:
                        scores_last(u + 2, i)

            def attention(i):
                slow = is_slow(nc.vector, i)
                with dve.If(slow != 0):
                    attention_all(i)
                with dve.Else():
                    attention_last(i)

            def step(ins, own, n, apart=False):
                ins.then_inc(own, 1)
                (wait_apart if apart else type(dve).wait_ge)(dve, own, n)

            def context_in(i, j):
                dve.wait_ge(pe_ctxT, NB * i + j + 1)
                nc.vector.tensor_copy(ctxT[:, j, :].rearrange("p (a n) -> p a n", a=3),
                                      ps[:, SET[0]:SET[0] + 3, 0:500]).then_inc(v_ctxT, 1)

            def queries0(i):
                n = 3 + A_STEPS * i
                dve.wait_ge(pe_xT, i + 1)
                nc.vector.tensor_copy(xT[:, :, :].rearrange("p t n -> p (t n)"), ps[:, XTB, :]).then_inc(v_xT, 1)
                dve.wait_ge(pe_q0, i + 1)
                nc.vector.tensor_scalar(q0T[:, :], ps[:, Q0B, 0:TP], float(D) ** -0.5, None,
                                        ALU.mult).then_inc(v_q0, 1)
                dve.wait_ge(pe_zx, i + 1)
                for p in range(PAIRS):
                    step(nc.vector.tensor_tensor(ya[:, p, :], ps[:, ZXB, p * D:(p + 1) * D], bgate_bc[:, :],
                                                 ALU.add), v_step, n + p + 1)

            def moments(src, st, own, n, done):
                for p in range(PAIRS):
                    ins = nc.vector.bn_stats(bst[st][:, p, :], src[:, p, :])
                step(ins, own, n, apart=True)
                for p in range(PAIRS):
                    ins = nc.vector.bn_aggr(mv[st][:, p, :], bst[st][:, p, :])
                ins.then_inc(done, 1)

            def hats(dst, src, st, done):
                for p in range(PAIRS):
                    ins = nc.vector.tensor_scalar(dst[:, p, :], src[:, p, :], mv[st][:, p, 0:1], rstd[st][:, p:p + 1],
                                                  ALU.subtract, ALU.mult)
                ins.then_inc(done, 1)

            def scale_shift(dst, bank, gb, done):
                for t in range(DT):
                    ins = nc.vector.tensor_scalar(dst[:, t, :], ps[:, bank, t * TP:(t + 1) * TP],
                                                  gb[:, 0, t:t + 1], gb[:, 1, t:t + 1], ALU.mult, ALU.add)
                ins.then_inc(done, 1)

            def front(i):
                n = 3 + A_STEPS * i
                for p in range(PAIRS):
                    dve.wait_ge(pe_s0, PAIRS * i + p + 1)
                    nc.vector.tensor_reduce(nmax0[:, p:p + 1], ps[:, SET[p]:SET[p] + 3, 0:500], AX.XY, ALU.max,
                                            negate=True).then_inc(v_max0, 1)
                dve.wait_ge(pe_p0T, PAIRS * i + 1)
                nc.vector.tensor_copy(p0T[0:KP, 0, :],
                                      ps[0:KP, SET[0]:SET[0] + 3, :].rearrange("p a n -> p (a n)")).then_inc(v_p0T, 1)
                dve.wait_ge(a_p0, PAIRS * i + PAIRS)
                step(nc.vector.reciprocal(rsum0[:, :], sum0[:, :]), v_step, n + 3)
                dve.wait_ge(pe_c0, i + 1)
                nc.vector.tensor_copy(c0T[:, :], ps[:, C0B, 0:TP]).then_inc(v_c0, 1)
                for p in range(PAIRS):
                    dve.wait_ge(pe_mz, PAIRS * i + p + 1)
                    nc.vector.scalar_tensor_tensor(out=ya[:, p, :], in0=ps[:, SET[p], D:2 * D],
                                                   scalar=rsum0[:, p:p + 1], in1=ya[:, p, :],
                                                   op0=ALU.mult, op1=ALU.add).then_inc(v_z, 1)
                dve.wait_ge(a_z, i + 1)
                step(nc.vector.tensor_scalar(yb[:, :, :], yb[:, :, :], 1.0, None, ALU.add), v_step, n + 4)
                step(nc.vector.reciprocal(yb[:, :, :], yb[:, :, :]), v_step, n + 5)
                for p in range(PAIRS):
                    ins = nc.vector.scalar_tensor_tensor(out=yb[:, p, :], in0=ps[:, SET[p], 0:D],
                                                         scalar=rsum0[:, p:p + 1], in1=yb[:, p, :],
                                                         op0=ALU.mult, op1=ALU.mult)
                step(ins, v_step, n + 6)
                step(nc.vector.tensor_tensor(yb[:, :, :], yb[:, :, :], xn[:, :, :], ALU.add), v_step, n + 7)
                for p in range(PAIRS):
                    ins = nc.vector.tensor_tensor_reduce(out=ya[:, p, :], in0=yb[:, p, :], in1=yb[:, p, :],
                                                         scale=1.0, scalar=0.0, op0=ALU.mult, op1=ALU.add,
                                                         accum_out=ssq[:, p:p + 1])
                ins.then_inc(v_stat, 1)
                dve.wait_ge(p_stat, 2 * i + 1)
                for p in range(PAIRS):
                    ins = nc.vector.scalar_tensor_tensor(out=x1[:, p, :], in0=yb[:, p, :],
                                                         scalar=rstd[0][:, p:p + 1], in1=normw_bc[:, :],
                                                         op0=ALU.mult, op1=ALU.mult)
                ins.then_inc(v_x1, 1)
                dve.wait_ge(v_x1, i + 1)
                moments(x1, 0, v_step, n + 8, v_stat)
                dve.wait_ge(v_stat, 2 * i + 2)
                dve.wait_ge(p_stat, 2 * i + 2)
                hats(yb, x1, 0, v_hat)

            def queries_in(i):
                dve.wait_ge(pe_hatT, i + 1)
                scale_shift(lnT, HATA, lnq_gb, v_lnT)
                for hp in range(1, H // 2, 2):
                    dve.wait_ge(pe_q, 8 * i + hp + 1)
                    nc.vector.tensor_copy(
                        qT[:, :, 2 * hp:2 * hp + 2, :].rearrange("p b h s -> p h b s"),
                        ps[:, QB[hp % 4], 0:2 * T4].rearrange("p (h b s) -> p h b s", h=2, s=S)).then_inc(v_q, 1)

            def tail_in(i):
                for p in range(PAIRS):
                    dve.wait_ge(pe_att, PAIRS * i + p + 1)
                    ins = nc.vector.tensor_tensor(x2[:, p, :], ps[:, ATT[p], 0:D], x1[:, p, :], ALU.add)
                ins.then_inc(v_x2, 1)
                dve.wait_ge(v_x2, i + 1)
                moments(x2, 1, v_stepd, D_STEPS * i + 1, v_statd)

            def tail_hats(i):
                dve.wait_ge(out_st, 16 * NB * i + 16)
                dve.wait_ge(v_statd, i + 1)
                dve.wait_ge(p_statd, i + 1)
                hats(yd, x2, 1, v_hatd)

            def tail_rows(i):
                dve.wait_ge(pe_hatdT, i + 1)
                scale_shift(ffT, HATD, lnf_gb, v_ffT)

            def tail_out(i):
                for p in range(PAIRS):
                    dve.wait_ge(pe_y, PAIRS * i + p + 1)
                    ins = nc.vector.tensor_tensor(yd[:, p, :], ps[:, YB[p], 0:D], x2[:, p, :], ALU.add)
                ins.then_inc(v_out, 1)

            dve.sem_inc(v_out, 1)
            context_in(0, 0)
            context_in(0, 2)
            queries0(0)
            front(0)
            queries_in(0)
            with dve.Fori(0, BLOCKS - 1) as i:
                attention(i)
                context_in(i + 1, 0)
                tail_in(i)
                context_in(i + 1, 2)
                tail_hats(i)
                queries0(i + 1)
                tail_rows(i)
                front(i + 1)
                tail_out(i)
                queries_in(i + 1)
            attention(BLOCKS - 1)
            tail_in(BLOCKS - 1)
            tail_hats(BLOCKS - 1)
            tail_rows(BLOCKS - 1)
            tail_out(BLOCKS - 1)

        @block.tensor
        def _(pe):
            mm, tr = nc.tensor.matmul, nc.tensor.transpose
            pe.wait_ge(p_const, 1)
            pe.wait_ge(wts_in, 16 * 15)
            for t in range(2):
                for k in range(2):
                    for j in range(4):
                        c = 4 * k + j
                        ins = tr(ps[:, 2 * t + k, j * 128:(j + 1) * 128], wq_n[:, t, c * 128:(c + 1) * 128], ident[:, :])
                    ins.then_inc(pe_w, 1)
            for k in range(4):
                for j in range(4):
                    c = 4 * k + j
                    ins = tr(ps[:, 4 + k, j * 128:(j + 1) * 128], wkv_n[:, c * 128:(c + 1) * 128], ident[:, :])
                ins.then_inc(pe_w, 1)
            for half in range(2):
                pe.wait_ge(v_w, half + 1)
                for f in range(DT):
                    for o in range(DT):
                        c = DT * half + f
                        ins = tr(ps[:, half, f * D + o * 128:f * D + (o + 1) * 128],
                                 wgate_n[:, o, c * 128:(c + 1) * 128], ident[:, :])
                ins.then_inc(pe_w, 1)
            pe.wait_ge(v_w, 3)
            for t in range(DT):
                ins = tr(ps[:, 2, t * 128:(t + 1) * 128], wmem[:, t, :], ident[:, :])
            ins.then_inc(pe_w, 1)
            pe.wait_ge(v_w, 10)
            for t in range(DT):
                ins = mm(ps[:, 3, 0:D], wmem[:, t, :], wgcT[:, t, :], start=(t == 0), stop=(t == DT - 1))
            ins.then_inc(pe_w, 1)
            pe.wait_ge(v_w, 12)
            for par in range(2):
                for j in range(H // 2):
                    rows = slice(64 * par, 64 * par + 64)
                    ins = mm(ps[:, 4 * par + j // 2, (j % 2) * D:(j % 2 + 1) * D], wkvT[rows, 8 + j, :],
                             wo_n[rows, j, :], start=True, stop=True)
                ins.then_inc(pe_w, 1)
            for k in range(4):
                pe.wait_ge(v_w, 13 + k // 2)
                for par in range(2):
                    rows = slice(64 * par, 64 * par + 64)
                    for t in range(DT):
                        for jj in range(2):
                            j = 2 * k + jj
                            c0 = (2 * t + jj) * E
                            ins = mm(ps[:, 2 * k + par, c0:c0 + E], wqT[rows, j, t * 128:(t + 1) * 128],
                                     wkvT[rows, j, :], start=True, stop=True)
                ins.then_inc(pe_w, 1)
            pe.wait_ge(flag_in, 16)
            pe.wait_ge(v_slow, 1)
            pe.wait_ge(v_w, 19)
            pe.wait_ge(p_const, 4)

            def score_matmul(u, c, gg):
                b, h0 = u // UPB, 4 * (u % UPB) + 2 * gg
                return mm(ps[0:G, gg, 0:CH], qT[:, b, h0:h0 + 2, :].rearrange("p h s -> p (h s)"),
                          ctxT[:, b, c * CH:(c + 1) * CH], start=True, stop=True)

            def transpose_probs(u, c):
                r, slot = u % RING, (u + c) % 2
                for t in range(KT):
                    for gg in range(2):
                        col = (t % 2) * 256 + gg * G
                        ins = tr(ps[0:KP, 2 + 2 * slot + t // 2, col:col + G],
                                 scores[0:G, r, gg, c * CH + t * KP:c * CH + (t + 1) * KP], ident[0:G, 0:G])
                return ins

            def unit_scores(u, i, live):
                b = u // UPB
                n, m = PS * (UNITS * i + u), VS * (UNITS * i + u)
                if u % UPB == 0:
                    live[b] = chunk_flags(nc.tensor, i, b)
                for c in range(NCH):
                    with pe.If(live[b][c] != 0):
                        for gg in range(2):
                            if c:
                                pe.wait_ge(v_s, m + 2 * c - 1 + gg)
                            elif u:
                                pe.wait_ge(v_s, m)
                            score_matmul(u, c, gg).then_inc(pe_s, 1)
                    with pe.Else():
                        if u or c:
                            pe.wait_ge(pe_s, n + 2 * c)
                        pe.sem_inc(pe_s, 2)

            def unit_pT(u, i, live):
                b = u // UPB
                n = NCH * (UNITS * i + u)
                for c in range(NCH):
                    with pe.If(live[b][c] != 0):
                        pe.wait_ge(v_prob, n + c + 1)
                        if c == 1 and u:
                            pe.wait_ge(a_pT, n - 1)
                        elif c != 1 and (u or c):
                            pe.wait_ge(a_pT, n + max(c - 1, 0))
                        transpose_probs(u, c).then_inc(pe_pT, 1)
                    with pe.Else():
                        if u or c:
                            pe.wait_ge(pe_pT, n + c)
                        pe.sem_inc(pe_pT, 1)
                    if c < NCH - 1:
                        unit_pv(u, c, i, live)

            def unit_pv(u, c, i, live):
                b, slot = u // UPB, (u + c) % 2
                if c == 0:
                    if u >= 2:
                        pe.wait_ge(a_o, UNITS * i + u - 1)
                    mm(ps[:, 6 + u % 2, 0:U], zeros[0:1, :], any_row(b), start=True, stop=False,
                       skip_group_check=True)
                with pe.If(live[b][c] != 0):
                    pe.wait_ge(a_pT, NCH * (UNITS * i + u) + c + 1)
                    for t in range(KT):
                        mm(ps[:, 6 + u % 2, 0:U], ctx[:, b, KT * c + t, :], pT[:, slot, t, :],
                           start=False, stop=False, skip_group_check=True)

            def any_row(b):
                return ctx[0:1, b, 0:2, :].rearrange("p t e -> p (t e)")[:, 0:U]

            def attention_all(i):
                live = {}
                unit_scores(0, i, live)
                unit_scores(1, i, live)
                for u in range(UNITS):
                    unit_pT(u, i, live)
                    if u + 2 < UNITS:
                        unit_scores(u + 2, i, live)
                    unit_pv(u, NCH - 1, i, live)
                    mm(ps[:, 6 + u % 2, 0:U], zeros[0:1, :], any_row(u // UPB), start=False, stop=True,
                       skip_group_check=True).then_inc(pe_o, 1)

            def last_scores(u, i):
                for gg in range(2):
                    if u:
                        pe.wait_ge(v_s, VS * (UNITS * i + u - 1) + VS // 2 * (gg + 1))
                    score_matmul(u, NCH - 1, gg).then_inc(pe_s, PS // 2)

            def attention_last(i):
                last_scores(0, i)
                last_scores(1, i)
                for u in range(UNITS):
                    b, slot = u // UPB, (u + NCH - 1) % 2
                    pe.wait_ge(v_prob, NCH * (UNITS * i + u + 1))
                    if u >= 2:
                        pe.wait_ge(a_pT, NCH * (UNITS * i + u - 1))
                    transpose_probs(u, NCH - 1).then_inc(pe_pT, NCH)
                    if u + 2 < UNITS:
                        last_scores(u + 2, i)
                    pe.wait_ge(a_pT, NCH * (UNITS * i + u + 1))
                    if u >= 2:
                        pe.wait_ge(a_o, UNITS * i + u - 1)
                    for t in range(KT):
                        ins = mm(ps[:, 6 + u % 2, 0:U], ctx[:, b, KT * (NCH - 1) + t, :], pT[:, slot, t, :],
                                 start=(t == 0), stop=(t == KT - 1))
                    ins.then_inc(pe_o, 1)

            def attention(i):
                pe.wait_ge(v_out, i + 1)
                slow = is_slow(nc.tensor, i)
                with pe.If(slow != 0):
                    attention_all(i)
                with pe.Else():
                    attention_last(i)

            def context_T(i, j):
                pe.wait_ge(ctx_in_s[j], 16 * i + 16)
                if j >= 2:
                    pe.wait_ge((v_ctxT, a_ctxT)[j % 2], 2 * i + 1)
                for t in range(NT):
                    ins = tr(ps[:, SET[j % 2] + t // 4, (t % 4) * KP:(t % 4 + 1) * KP], ctx[:, j, t, :],
                             ident[0:KP, 0:KP])
                ins.then_inc(pe_ctxT, 1)

            def row_transposes(bank, src):
                for t in range(DT):
                    for p in range(PAIRS):
                        ins = tr(ps[:, bank, t * TP + p * 128:t * TP + (p + 1) * 128],
                                 src[:, p, t * 128:(t + 1) * 128], ident[:, :])
                return ins

            def queries0(i):
                pe.wait_ge(x_in, 16 * NB * i + 16 * NB)
                pe.wait_ge(v_ctxT, 2 * i + 2)
                row_transposes(XTB, xn).then_inc(pe_xT, 1)
                pe.wait_ge(v_xT, i + 1)
                for t in range(DT):
                    ins = mm(ps[:, Q0B, 0:TP], wmem[:, t, :], xT[:, t, :], start=(t == 0), stop=(t == DT - 1))
                ins.then_inc(pe_q0, 1)
                for p in range(PAIRS):
                    for t in range(DT):
                        ins = mm(ps[:, ZXB, p * D:(p + 1) * D], xT[:, t, p * 128:(p + 1) * 128], wgx[:, t, :],
                                 start=(t == 0), stop=(t == DT - 1))
                ins.then_inc(pe_zx, 1)

            def layer0(i):
                pe.wait_ge(v_q0, i + 1)
                pe.wait_ge(v_step, 3 + A_STEPS * i + 2)
                pe.wait_ge(a_ctxT, 2 * i + 2)
                for p in range(PAIRS):
                    for k in range(3):
                        for hb in range(2):
                            j = 2 * p + hb
                            ins = mm(ps[SP * hb:SP * hb + SP, SET[p] + k, 0:500], q0T[:, j * SP:(j + 1) * SP],
                                     ctxT[:, j, k * 500:(k + 1) * 500], start=True, stop=True)
                    ins.then_inc(pe_s0, 1)
                for p in range(PAIRS):
                    pe.wait_ge(a_p0, PAIRS * i + p + 1)
                    for t in range(NT):
                        ins = tr(ps[0:KP, SET[p] + t // 4, (t % 4) * 128:(t % 4 + 1) * 128],
                                 p0[:, p, t * KP:(t + 1) * KP], ident[:, :])
                    ins.then_inc(pe_p0T, 1)
                for p in range(PAIRS):
                    pe.wait_ge(v_p0T if p == 0 else a_p0T, i + 1)
                    for hb in range(2):
                        j = 2 * p + hb
                        for t in range(NT):
                            ins = mm(ps[:, C0B, j * SP:(j + 1) * SP], ctx[:, j, t, :],
                                     p0T[0:KP, p, t * 128 + hb * SP:t * 128 + hb * SP + SP],
                                     start=(t == 0), stop=(t == NT - 1))
                ins.then_inc(pe_c0, 1)
                pe.wait_ge(v_c0, i + 1)
                for p in range(PAIRS):
                    mm(ps[:, SET[p], :], c0T[:, p * 128:(p + 1) * 128],
                       wmz[:, :, :].rearrange("p a n -> p (a n)"), start=True, stop=True).then_inc(pe_mz, 1)

            def unpadded(rows):
                return [rows[:, t, :].rearrange("p (b s) -> p b s", s=SP)[:, :, 0:S] for t in range(DT)]

            def queries1(i):
                pe.wait_ge(v_hat, i + 1)
                row_transposes(HATA, yb).then_inc(pe_hatT, 1)
                pe.wait_ge(v_lnT, i + 1)
                tok = unpadded(lnT)
                for hp in range(H // 2):
                    if hp >= 4:
                        pe.wait_ge((a_q, v_q)[hp % 2], 4 * i + (hp - 4) // 2 + 1)
                    for h in range(2):
                        for t in range(DT):
                            ins = mm(ps[:, QB[hp % 4], h * T4:(h + 1) * T4], wqk[:, t, 2 * hp + h, :], tok[t],
                                     start=(t == 0), stop=(t == DT - 1))
                    ins.then_inc(pe_q, 1)
                pe.wait_ge(a_q, 4 * i + 4)
                pe.wait_ge(v_q, 4 * i + 4)

            def attention_out(i):
                pe.wait_ge(a_o, UNITS * i + UNITS)
                for p in range(PAIRS):
                    for h in range(H):
                        ins = mm(ps[:, ATT[p], 0:D], oT[:, h, 2 * p:2 * p + 2, :].rearrange("p b s -> p (b s)"),
                                 wvo[:, h, :], start=(h == 0), stop=(h == H - 1))
                    ins.then_inc(pe_att, 1)

            def hidden(i):
                pe.wait_ge(v_hatd, i + 1)
                row_transposes(HATD, yd).then_inc(pe_hatdT, 1)
                pe.wait_ge(v_ffT, i + 1)
                tok = unpadded(ffT)
                for k in range(FT // 2):
                    if k >= 2:
                        pe.wait_ge(a_gelu, 4 * i + k - 1)
                    for f in range(2):
                        ft = 2 * k + f
                        for t in range(DT):
                            ins = mm(ps[:, W1B[k % 2], f * T4:(f + 1) * T4], w1_sb[:, t, ft * 128:(ft + 1) * 128],
                                     tok[t], start=(t == 0), stop=(t == DT - 1))
                    ins.then_inc(pe_h, 1)
                pe.wait_ge(a_gelu, 4 * i + 4)

            def feed_forward_out(i):
                pe.wait_ge(p_pad, i + 1)
                for p in range(PAIRS):
                    for f in range(FT):
                        ins = mm(ps[:, YB[p], 0:D], h1T[:, f, 2 * p:2 * p + 2, :].rearrange("p b s -> p (b s)"),
                                 w2_sb[:, f, :], start=(f == 0), stop=(f == FT - 1))
                    ins.then_inc(pe_y, 1)

            for j in range(NB):
                context_T(0, j)
            queries0(0)
            layer0(0)
            queries1(0)
            with pe.Fori(0, BLOCKS - 1) as i:
                attention(i)
                pe.wait_ge(a_o, UNITS * i + UNITS)
                context_T(i + 1, 0)
                context_T(i + 1, 1)
                attention_out(i)
                context_T(i + 1, 2)
                context_T(i + 1, 3)
                queries0(i + 1)
                hidden(i)
                layer0(i + 1)
                feed_forward_out(i)
                queries1(i + 1)
            attention(BLOCKS - 1)
            attention_out(BLOCKS - 1)
            hidden(BLOCKS - 1)
            feed_forward_out(BLOCKS - 1)


_INS = ['x', 'ctx_1024', 'mask_BxS2_bk0', 'L0_xattn_W_mem', 'L0_xattn_W_gate', 'L0_xattn_b_gate',
        'L0_xattn_norm_w', 'L1_xattn_ln_q_g', 'L1_xattn_ln_q_b', 'L1_xattn_Wq', 'L1_xattn_Wkv', 'L1_xattn_Wo',
        'L1_xattn_attn_gate', 'L1_xattn_ln_ff_g', 'L1_xattn_ln_ff_b', 'L1_xattn_W1', 'L1_xattn_W2',
        'L1_xattn_ff_gate']


def kernel(**inputs):
    import numpy as _np
    import concourse.bacc as _bacc
    from concourse import mybir as _mybir
    from concourse.bass_utils import run_bass_kernel_spmd as _run

    nc = _bacc.Bacc("TRN2", target_bir_lowering=False, num_devices=1)
    arrays, args = {}, []
    for name in _INS:
        a = _np.ascontiguousarray(inputs[name])
        arrays[f"in_{name}_dram"] = a
        args.append(nc.dram_tensor(f"in_{name}_dram", a.shape, _mybir.dt.from_np(a.dtype), kind="ExternalInput").ap())
    shape = inputs['x'].shape
    args.append(nc.dram_tensor("out_0_dram", shape, _mybir.dt.float32, kind="ExternalOutput").ap())
    xattn_kernel(nc, *args)
    r = _run(nc, [arrays], core_ids=[0])
    return r.results[0]["out_0_dram"]
```

```python
import concourse.bass as bass
from concourse import mybir
from contextlib import ExitStack


def xattn_kernel(nc, x, ctx_in, mask, w_mem, w_gate, b_gate, norm_w, ln_q_g, ln_q_b, wq, wkv, wo,
                 attn_gate, ln_ff_g, ln_ff_b, w1, w2, ff_gate, out):
    fp32, u8, i32 = mybir.dt.float32, mybir.dt.uint8, mybir.dt.int32
    f32r = mybir.dt.float32r
    ALU, ACT, AX = mybir.AluOpType, mybir.ActivationFunctionType, mybir.AxisListType

    B, S, D = x.shape
    M, E = ctx_in.shape[1:]
    INNER = wq.shape[1]
    DH = 64
    H = INNER // DH
    F = w1.shape[1]
    NB = 4
    BLOCKS = B // NB
    PAIRS = NB // 2
    SP = 64
    TP = NB * SP
    DT = D // 128
    FT = F // 128
    NCH = 4
    CH = M // NCH
    ODD = CH % 2
    LAST = M - CH
    KT = 3
    KP = CH // KT
    NT = NCH * KT
    G = 2 * S
    U = 2 * G
    UPB = H // 4
    UNITS = NB * UPB
    RING = 3
    T4 = NB * S
    NEG = -3.4028234663852886e38
    EPS0, EPS1 = 1e-6, 1e-5
    PS, VS = 2 * NCH, 2 * NCH + 2

    with ExitStack() as stack:
        def sb(name, shape, dt=fp32):
            return stack.enter_context(nc.sbuf_tensor(name, shape, dt))

        def lent(name, shape, dt):
            with nc.sbuf_tensor(name, shape, dt) as t:
                return t

        def sem(name):
            return stack.enter_context(nc.semaphore(name))

        wqk = sb("wqk", [128, DT, H, E])
        wv_sb = sb("wv_sb", [128, H, DH])
        wo_sb = sb("wo_sb", [128, H // 2, D])
        w1_sb = sb("w1_sb", [128, DT, F])
        w2_sb = sb("w2_sb", [128, FT, D])
        wmem = sb("wmem", [128, DT, E])
        wgx = sb("wgx", [128, DT, D])
        wmz = sb("wmz", [128, 2, D])
        bgate_bc = sb("bgate_bc", [128, D])
        normw_bc = sb("normw_bc", [128, D])
        lnq_gb = sb("lnq_gb", [128, 2, DT])
        lnf_gb = sb("lnf_gb", [128, 2, DT])
        gates = sb("gates", [128, 4])
        ident = sb("ident", [128, 128])
        neg_half = sb("neg_half", [128, 2])
        zeros = sb("zeros", [1, 128])
        flag_row = sb("flag_row", [1, B * NCH], i32)
        slow_row = sb("slow_row", [1, BLOCKS], i32)
        ctx = sb("ctx", [KP, NB, NT, E])
        ctxT = sb("ctxT", [128, NB, M])
        xn = sb("xn", [128, PAIRS, D])
        xT = sb("xT", [128, DT, TP])
        q0T = sb("q0T", [128, TP])
        x1 = sb("x1", [128, PAIRS, D])
        x2 = sb("x2", [128, PAIRS, D])
        ffT = sb("ffT", [128, DT, TP])
        ya = sb("ya", [128, PAIRS, D])
        yb = sb("yb", [128, PAIRS, D])
        yd = sb("yd", [128, PAIRS, D])
        q_hi = lent("q_hi", [128, H // 2, NB, SP, 2], f32r)
        oT = sb("oT", [128, H // 2, NB, SP, 2])
        q_lo = sb("q_lo", [128, NB, H // 2, S, 2], f32r)
        cT_parts = lent("cT_parts", [128, NB, 1536], f32r)
        cT_hi, cT_lo = [cT_parts[:, :, k * (CH + ODD):(k + 1) * (CH + ODD)] for k in range(2)]
        scores = sb("scores", [128, RING, 2, 1536])
        pT = sb("pT", [KP, 2, KT, U])
        mask_u8 = sb("mask_u8", [G, 2, M], u8)
        mbias = sb("mbias", [G, 2, M])
        nmax0 = sb("nmax0", [128, PAIRS])
        sum0 = sb("sum0", [128, PAIRS])
        rsum0 = sb("rsum0", [128, PAIRS])
        ssq = sb("ssq", [128, PAIRS])
        vpe = [sb(f"vpe{k}", [128, PAIRS]) for k in range(2)]
        rstd = [sb(f"rstd{k}", [128, PAIRS]) for k in range(2)]
        bst = [sb(f"bst{k}", [128, PAIRS, 6]) for k in range(2)]
        mv = [sb(f"mv{k}", [128, PAIRS, 2]) for k in range(2)]
        cmin = sb("cmin", [G, RING, 2, NCH])
        nmax = sb("nmax", [G, RING, 2])
        sums = sb("sums", [G, RING, 2, NCH])
        tsum = sb("tsum", [G, RING, 2])
        rsum = sb("rsum", [G, RING, 2])
        any_f = sb("any_f", [B, NCH])
        none_f = sb("none_f", [B, 1])
        flags = sb("flags", [B, NCH], i32)
        ring2 = scores[:, 2, :, :].rearrange("p a n -> p (a n)")
        heads = oT.rearrange("p k b s h -> p (k b s h)")
        wq_n = w1_sb
        wk_n = w2_sb.rearrange("p f n -> p (f n)")[:, 0:INNER]
        wgate_n = ring2[:, 0:DT * 2 * D].rearrange("p (t n) -> p t n", t=DT)
        wkT = ring2[:, DT * 2 * D:DT * 2 * D + 8 * E].rearrange("p (j n) -> p j n", j=8)
        wqT = heads[:, 0:8 * D].rearrange("p (j n) -> p j n", j=8)
        wgcT = x2
        mask_rows = mask_u8[0:B, 0, :]
        p0 = scores[:, 0, :, :]
        p0T = scores[:, 1, :, :]
        lnT, c0T = xT, q0T
        h1T = scores[:, 2, :, :].rearrange("p g n -> p (g n)")[:, 0:FT * TP].rearrange(
            "p (f b s) -> p f b s", f=FT, b=NB)
        vT = h1T

        ps = stack.enter_context(nc.psum_tensor("ps", [128, 8, 512], fp32))
        SET = (2, 5)
        XTB, Q0B, ZXB, ATT = 0, 1, 0, (0, 1)
        C0B, C0TB, HATD, HATA = (0, 1), 0, (6, 7), (6, 7)
        VB = (0, 1, 0, 1)
        W1B, MZB, YB = (2, 3, 7, 6), (4, 5), (0, 1)
        QB = (2, 3, 4, 5, 2, 3, 6, 7)

        wgate_in, wmem_in, wq_in, wk_in, wv_in, wo_in, w1_in, w2_in = [
            sem(n) for n in ("wgate_in", "wmem_in", "wq_in", "wk_in", "wv_in", "wo_in", "w1_in", "w2_in")]
        bgate_in = sem("bgate_in")
        vec_in = sem("vec_in")
        mrow_in = sem("mrow_in")
        flag_in = sem("flag_in")
        ctx_in_s = [sem(f"ctx_in{j}") for j in range(NB)]
        x_in = sem("x_in")
        mask_in = [sem(f"mask_in{k}") for k in range(2)]
        out_st = sem("out_st")
        p_const = sem("p_const")
        p_mask = sem("p_mask")
        p_stat = sem("p_stat")
        p_pad = sem("p_pad")
        p_step = sem("p_step")
        pe_w = sem("pe_w")
        v_w = sem("v_w")
        a_w = sem("a_w")
        v_gated = sem("v_gated")
        v_step = sem("v_step")
        v_bns = sem("v_bns")
        v_bnsd = sem("v_bnsd")
        a_gate = sem("a_gate")
        v_flag = sem("v_flag")
        pe_ctxT = sem("pe_ctxT")
        v_ctxT = sem("v_ctxT")
        a_ctxT = sem("a_ctxT")
        pe_xT = sem("pe_xT")
        v_xT = sem("v_xT")
        pe_q0 = sem("pe_q0")
        v_q0 = sem("v_q0")
        pe_zx = sem("pe_zx")
        v_zx = sem("v_zx")
        pe_s0 = sem("pe_s0")
        v_max0 = sem("v_max0")
        a_p0 = sem("a_p0")
        pe_p0T = sem("pe_p0T")
        v_p0T = sem("v_p0T")
        a_p0T = sem("a_p0T")
        pe_c0 = sem("pe_c0")
        v_rs0 = sem("v_rs0")
        v_c0 = sem("v_c0")
        pe_c0T = sem("pe_c0T")
        v_c0T = sem("v_c0T")
        pe_mz = sem("pe_mz")
        v_z = sem("v_z")
        a_z = sem("a_z")
        v_t1 = sem("v_t1")
        v_fused = sem("v_fused")
        a_ssq = sem("a_ssq")
        p_rms = sem("p_rms")
        v_slow = sem("v_slow")
        v_stat = sem("v_stat")
        v_statd = sem("v_statd")
        p_statd = sem("p_statd")
        p_stepd = sem("p_stepd")
        v_x2 = sem("v_x2")
        v_hatd = sem("v_hatd")
        pe_hatdT = sem("pe_hatdT")
        v_ffT = sem("v_ffT")
        a_ffT = sem("a_ffT")
        v_x1 = sem("v_x1")
        v_hat = sem("v_hat")
        pe_hatT = sem("pe_hatT")
        v_lnT = sem("v_lnT")
        a_lnT = sem("a_lnT")
        pe_q = sem("pe_q")
        a_q = sem("a_q")
        v_q = sem("v_q")
        a_cT = sem("a_cT")
        v_cT = sem("v_cT")
        pe_s = sem("pe_s")
        v_s = sem("v_s")
        a_exp = sem("a_exp")
        v_prob = sem("v_prob")
        v_rs = sem("v_rs")
        pe_pT = sem("pe_pT")
        a_pT = sem("a_pT")
        pe_o = sem("pe_o")
        a_o = sem("a_o")
        pe_v = sem("pe_v")
        a_v = sem("a_v")
        pe_att = sem("pe_att")
        pe_h = sem("pe_h")
        a_gelu = sem("a_gelu")
        pe_y = sem("pe_y")
        v_out = sem("v_out")

        T_STEP, K_STEP = list(range(1, 7)), list(range(7, 15))

        block = stack.enter_context(nc.Block())

        ctx_v = ctx_in.rearrange("(i j) (c p t) e -> i j p c (t e)", j=NB, c=NCH, t=KT)
        x_v = x.rearrange("(i b) s d -> i b s d", b=NB)
        out_v = out.rearrange("(i b) s d -> i b s d", b=NB)
        mask_v = mask.rearrange("(i b) m -> i b m", b=NB)

        def chunk_flags(eng, i, b):
            return [eng.value_load(flag_row[0:1, bass.ds(NB * NCH * i + NCH * b + c, 1)], min_val=0, max_val=1)
                    for c in range(NCH)]

        def wait_apart(eng, sem, value):
            held = eng.compute_val(value)
            eng.wait_ge(flag_in, 16)
            eng.wait_ge(sem, held)

        def is_slow(eng, i):
            return eng.value_load(slow_row[0:1, bass.ds(i, 1)], min_val=0, max_val=1)

        def row_bc(v, parts):
            return bass.AP(v.tensor, v.offset, [[0, parts], [1, v.shape[0]]])

        def load_ctx(eng, i, j):
            eng.dma_start(ctx[:, j, :, :].rearrange("p (c t) e -> p c (t e)", t=KT),
                          ctx_v[i, j]).then_inc(ctx_in_s[j], 16)

        def load_x(eng, i):
            for b in range(NB):
                eng.dma_start(xn[SP * (b % 2):SP * (b % 2) + S, b // 2, :], x_v[i, b]).then_inc(x_in, 16)

        def load_mask(eng, i, b):
            eng.dma_start(mask_u8[:, b % 2, :], bass.AP(mask_v.tensor, mask_v[i, b].offset, [[0, G], [1, M]])
                          ).then_inc(mask_in[b % 2], 16)

        @block.sync
        def _(sp):
            sp.dma_start(mask_rows, mask).then_inc(mrow_in, 16)
            sp.wait_ge(p_const, 3)
            load_x(sp, 0)
            load_ctx(sp, 0, 0)
            load_ctx(sp, 0, 1)
            sp.dma_start(wq_n[:, :, :], wq.rearrange("(t p) n -> p t n", p=128)).then_inc(wq_in, 16)
            load_ctx(sp, 0, 2)
            load_ctx(sp, 0, 3)
            sp.dma_start(wk_n, wkv[:, 0:INNER]).then_inc(wk_in, 16)
            sp.dma_start(wv_sb.rearrange("p h d -> p (h d)"), wkv[:, INNER:2 * INNER]).then_inc(wv_in, 16)
            sp.dma_start(wo_sb[:, :, :], wo.rearrange("(j p) n -> p j n", p=128)).then_inc(wo_in, 16)
            sp.wait_ge(v_flag, 1)
            load_mask(sp, 0, 0)
            load_mask(sp, 0, 1)
            sp.wait_ge(pe_w, 4 + T_STEP[-1])
            sp.dma_start(w1_sb[:, :, :], w1.rearrange("(t p) n -> p t n", p=128)).then_inc(w1_in, 16)
            sp.dma_start(w2_sb[:, :, :], w2.rearrange("(t p) n -> p t n", p=128)).then_inc(w2_in, 16)

            def store(i):
                for b in range(NB):
                    sp.dma_start(out_v[i, b], yd[SP * (b % 2):SP * (b % 2) + S, b // 2, :]).then_inc(out_st, 16)

            sp.sem_inc(out_st, 16)
            with sp.Fori(0, BLOCKS - 1) as i:
                for b in (2, 3):
                    wait_apart(sp, p_mask, NB * i + b - 1)
                    load_mask(sp, i, b)
                wait_apart(sp, v_x1, PAIRS * i + PAIRS)
                load_x(sp, i + 1)
                for j in range(NB):
                    if j >= 2:
                        wait_apart(sp, p_mask, NB * i + j + 1)
                        load_mask(sp, i + 1, j - 2)
                    wait_apart(sp, pe_o, UNITS * i + UPB * (j + 1))
                    load_ctx(sp, i + 1, j)
                wait_apart(sp, v_out, PAIRS * (i + 2))
                store(i)
            last = BLOCKS - 1
            for b in (2, 3):
                sp.wait_ge(p_mask, NB * last + b - 1)
                load_mask(sp, last, b)
            sp.wait_ge(v_out, PAIRS * (BLOCKS + 1))
            store(last)
            sp.wait_ge(out_st, 16 + 16 * NB * BLOCKS)

        @block.gpsimd
        def _(pool):
            nc.gpsimd.memset(ident[:, :], 0.0).then_inc(p_step, 1)
            pool.wait_ge(p_step, 1)
            nc.gpsimd.affine_select(out=ident[:, :], in_=ident[:, :], compare_op=ALU.not_equal, fill=1.0, base=0,
                                    pattern=[[-1, 128]], channel_multiplier=1).then_inc(p_const, 1)
            nc.gpsimd.memset(zeros[:, :], 0.0)
            nc.gpsimd.memset(neg_half[:, :], -0.5).then_inc(p_const, 1)
            nc.gpsimd.memset(xn[:, :, :], 0.0).then_inc(p_const, 1)
            pool.wait_ge(flag_in, 16)

            def rsqrt(src, mul, eps, stage, p, ready, n, own, m, done):
                wait_apart(pool, ready, n)
                nc.gpsimd.tensor_scalar(vpe[stage][:, p:p + 1], src, mul, eps, ALU.mult, ALU.add).then_inc(own, 1)
                wait_apart(pool, own, m)
                nc.gpsimd.tensor_tensor(rstd[stage][:, p:p + 1], vpe[stage][:, p:p + 1], neg_half[:, 0:1],
                                        ALU.pow).then_inc(done, 1)

            def front_stats(i):
                n, m = PAIRS * i + 1, 2 * PAIRS * i + 2
                for p in range(PAIRS):
                    rsqrt(ssq[:, p:p + 1], 1.0 / D, EPS0, 0, p, a_ssq, n + p, p_step, m + p, p_rms)
                for p in range(PAIRS):
                    rsqrt(mv[0][:, p, 1:2], 1.0, EPS1, 0, p, v_stat, n + p, p_step, m + PAIRS + p, p_stat)

            def tail_stats(i):
                n = PAIRS * i + 1
                for p in range(PAIRS):
                    rsqrt(mv[1][:, p, 1:2], 1.0, EPS1, 1, p, v_statd, n + p, p_stepd, n + p, p_statd)

            def mask_bias(i, b, after=None):
                if b >= 2:
                    wait_apart(pool, v_s, VS * (UNITS * i + UPB * (b - 1)))
                elif after is not None:
                    wait_apart(pool, v_s, VS * (UNITS * after + UPB * (b + 3)))
                wait_apart(pool, mask_in[b % 2], 32 * i + 16 * (b // 2) + 16)
                nc.gpsimd.tensor_scalar(
                    mbias[:, b % 2, :].rearrange("g (c t p) -> g c t p", c=NCH, t=KT),
                    mask_u8[:, b % 2, :].rearrange("g (c p t) -> g c t p", c=NCH, t=KT),
                    1.0, -NEG, ALU.subtract, ALU.mult).then_inc(p_mask, 1)

            mask_bias(0, 0)
            mask_bias(0, 1)
            front_stats(0)
            with pool.Fori(0, BLOCKS - 1) as i:
                mask_bias(i, 2)
                mask_bias(i, 3)
                mask_bias(i + 1, 0, after=i)
                mask_bias(i + 1, 1, after=i)
                wait_apart(pool, pe_o, UNITS * i + UNITS)
                nc.gpsimd.memset(h1T[:, :, :, S:SP], 0.0).then_inc(p_pad, 1)
                tail_stats(i)
                front_stats(i + 1)
            mask_bias(BLOCKS - 1, 2)
            mask_bias(BLOCKS - 1, 3)
            pool.wait_ge(pe_o, UNITS * BLOCKS)
            nc.gpsimd.memset(h1T[:, :, :, S:SP], 0.0).then_inc(p_pad, 1)
            tail_stats(BLOCKS - 1)

        @block.scalar
        def _(act):
            def load(dst, src, arrived, **kw):
                act.dma_start(dst, src, **kw).then_inc(arrived, 16)

            load(wgate_n, w_gate.rearrange("(t p) n -> p t n", p=128), wgate_in)
            load(wmem[:, :, :], w_mem.rearrange("(t p) n -> p t n", p=128), wmem_in)
            load(bgate_bc[:, :], row_bc(b_gate, 128), bgate_in)
            load(normw_bc[:, :], row_bc(norm_w, 128), vec_in)
            for k, (t, v) in enumerate([(lnq_gb, ln_q_g), (lnq_gb, ln_q_b), (lnf_gb, ln_ff_g), (lnf_gb, ln_ff_b)]):
                load(t[:, k % 2, :], v.rearrange("(t p) -> p t", p=128), vec_in, allow_slow_non_contiguous=True)
            load(gates[:, 0:1], row_bc(attn_gate, 128), vec_in)
            load(gates[:, 1:2], row_bc(ff_gate, 128), vec_in)
            act.wait_ge(v_flag, 1)
            act.dma_start(flag_row[0:1, :].rearrange("o (b c) -> o b c", c=NCH),
                          flags[:, :]).then_inc(flag_in, 16)
            act.wait_ge(vec_in, 16 * 7)
            nc.scalar.activation(gates[:, 2:4], gates[:, 0:2], ACT.Tanh).then_inc(a_gate, 1)

            def transposed_in(steps):
                for n in steps:
                    act.wait_ge(pe_w, 4 + T_STEP[n])
                    src = ps[:, n % 2, :].rearrange("p (j n) -> p j n", j=4)
                    if n < 4:
                        t, k = n // 2, n % 2
                        dst = wqT[:, 4 * k:4 * k + 4, t * 128:(t + 1) * 128]
                    else:
                        dst = wkT[:, 4 * (n - 4):4 * (n - 4) + 4, :]
                    nc.scalar.activation(dst, src, ACT.Copy).then_inc(a_w, 1)

            def wqk_in(steps):
                for m in steps:
                    k, par = m // 2, m % 2
                    act.wait_ge(pe_w, 4 + K_STEP[m])
                    h0 = 4 * k + par
                    nc.scalar.activation(wqk[:, :, h0:h0 + 3:2, :],
                                         ps[:, 2 + m % 2, :].rearrange("p (t h n) -> p t h n", t=DT, h=2),
                                         ACT.Copy, scale=0.125).then_inc(a_w, 1)

            def evac_o(u, i):
                b, k = u // UPB, u % UPB
                act.wait_ge(pe_o, UNITS * i + u + 1)
                nc.scalar.activation(oT[:, 2 * k:2 * k + 2, b, 0:S, :],
                                     ps[:, 6 + u % 2, 0:U].rearrange("p (g s h) -> p g s h", s=S, h=2),
                                     ACT.Copy).then_inc(a_o, 1)

            def exp_chunk(u, c):
                r = u % RING
                for gg in range(2):
                    v = scores[0:G, r, gg, c * CH:(c + 1) * CH]
                    ins = nc.scalar.activation(v, v, ACT.Exp, bias=nmax[:, r, gg:gg + 1], scale=-1.0,
                                               accum_out=sums[:, r, gg, c:c + 1])
                return ins

            def exps(u, i, live):
                if u % UPB == 0:
                    live[u // UPB] = chunk_flags(nc.scalar, i, u // UPB)
                wait_apart(act, v_s, VS * (UNITS * i + u + 1))
                for c in range(NCH):
                    with act.If(live[u // UPB][c] != 0):
                        exp_chunk(u, c).then_inc(a_exp, 1)
                    with act.Else():
                        if u or c:
                            act.wait_ge(a_exp, NCH * (UNITS * i + u) + c)
                        act.sem_inc(a_exp, 1)

            def copy_pT(u, c):
                slot = (u + c) % 2
                src = ps[0:KP, 2 + 2 * slot:4 + 2 * slot, :].rearrange("p a (z n) -> p (a z) n", z=2)[:, 0:KT, 0:U]
                return nc.scalar.activation(pT[:, slot, :, :], src, ACT.Copy)

            def evac_pT(u, i, live):
                for c in range(NCH):
                    slot = (u + c) % 2
                    wait_apart(act, pe_pT, NCH * (UNITS * i + u) + c + 1)
                    with act.If(live[u // UPB][c] != 0):
                        copy_pT(u, c).then_inc(a_pT, 1)
                    with act.Else():
                        if u or c:
                            act.wait_ge(a_pT, NCH * (UNITS * i + u) + c)
                        act.sem_inc(a_pT, 1)

            def attention_all(i):
                live = {}
                exps(0, i, live)
                exps(1, i, live)
                queries_in(i, range(4, 8))
                for u in range(UNITS):
                    evac_pT(u, i, live)
                    if u + 2 < UNITS:
                        exps(u + 2, i, live)
                    evac_o(u, i)

            def exps_last(u, i):
                r = u % RING
                act.wait_ge(v_s, VS * (UNITS * i + u + 1))
                for gg in range(2):
                    v = scores[0:G, r, gg, LAST:M]
                    ins = nc.scalar.activation(v, v, ACT.Exp, bias=cmin[:, r, gg, NCH - 1:NCH], scale=-1.0,
                                               accum_out=sums[:, r, gg, NCH - 1:NCH])
                ins.then_inc(a_exp, NCH)

            def attention_last(i):
                def evac_pT_last(u):
                    act.wait_ge(pe_pT, NCH * (UNITS * i + u + 1))
                    copy_pT(u, NCH - 1).then_inc(a_pT, NCH)

                exps_last(0, i)
                queries_in(i, (4,))
                exps_last(1, i)
                queries_in(i, range(5, 8))
                evac_pT_last(0)
                exps_last(2, i)
                for u in range(UNITS):
                    if u + 1 < UNITS:
                        evac_pT_last(u + 1)
                    if u + 3 < UNITS:
                        exps_last(u + 3, i)
                    evac_o(u, i)

            def attention(i):
                slow = is_slow(nc.scalar, i)
                queries_in(i, range(4))
                with act.If(slow != 0):
                    attention_all(i)
                with act.Else():
                    attention_last(i)

            def context_in(i, j):
                act.wait_ge(pe_ctxT, NB * i + j + 1)
                nc.scalar.activation(ctxT[:, j, :].rearrange("p (a n) -> p a n", a=3),
                                     ps[:, SET[1]:SET[1] + 3, 0:500], ACT.Copy).then_inc(a_ctxT, 1)

            def exp0(i, p):
                act.wait_ge(v_max0, PAIRS * i + p + 1)
                nc.scalar.activation(p0[:, p, 0:M].rearrange("p (a n) -> p a n", a=3),
                                     ps[:, SET[p]:SET[p] + 3, 0:500], ACT.Exp, bias=nmax0[:, p:p + 1],
                                     accum_out=sum0[:, p:p + 1]).then_inc(a_p0, 1)

            def probs0_in(i):
                act.wait_ge(pe_p0T, PAIRS * i + 2)
                nc.scalar.activation(p0T[0:KP, 1, :], ps[0:KP, SET[1]:SET[1] + 3, :].rearrange("p a n -> p (a n)"),
                                     ACT.Copy).then_inc(a_p0T, 1)

            def last_hi(i):
                act.wait_ge(pe_c0, PAIRS * i + PAIRS)
                nc.scalar.activation(cT_hi, ctxT[:, :, LAST - ODD:M], ACT.Copy).then_inc(a_cT, 1)

            def values_in(i, k):
                act.wait_ge(pe_v, 4 * i + k + 1)
                nc.scalar.activation(vT[:, 2 * k:2 * k + 2, :, 0:S],
                                     ps[:, VB[k], 0:2 * T4].rearrange("p (j b s) -> p j b s", j=2, s=S),
                                     ACT.Copy).then_inc(a_v, 1)

            def hidden_in(i, k):
                act.wait_ge(pe_h, 4 * i + k + 1)
                nc.scalar.activation(h1T[:, 2 * k:2 * k + 2, :, 0:S],
                                     ps[:, W1B[k], 0:2 * T4].rearrange("p (f b s) -> p f b s", f=2, s=S),
                                     ACT.Gelu).then_inc(a_gelu, 1)

            def gate_in(i):
                for p in range(PAIRS):
                    act.wait_ge(v_z, PAIRS * i + p + 1)
                    nc.scalar.activation(yb[:, p, :], ya[:, p, :], ACT.Tanh, scale=0.5).then_inc(a_z, 1)

            def squares(i):
                for p in range(PAIRS):
                    act.wait_ge(v_fused, PAIRS * i + p + 1)
                    nc.scalar.activation(ya[:, p, :], yb[:, p, :], ACT.Square,
                                         accum_out=ssq[:, p:p + 1]).then_inc(a_ssq, 1)

            def scale_shift(dst, banks, gb, ready, i, done):
                act.wait_ge(ready, i + 1)
                nc.scalar.activation(dst[:, 1, :], ps[:, banks[1], 0:TP], ACT.Identity, bias=gb[:, 1, 1:2],
                                     scale=gb[:, 0, 1:2]).then_inc(done, 1)

            def queries_in(i, pairs):
                for hp in pairs:
                    act.wait_ge(pe_q, 8 * i + hp + 1)
                    nc.scalar.activation(
                        q_hi[:, hp, :, 0:S, :].rearrange("p b s h -> p h b s"),
                        ps[:, QB[hp], 0:2 * T4].rearrange("p (h b s) -> p h b s", h=2, s=S),
                        ACT.Copy).then_inc(a_q, 1)

            context_in(0, 1)
            transposed_in(range(4))
            context_in(0, 3)
            transposed_in(range(4, 6))
            exp0(0, 0)
            exp0(0, 1)
            probs0_in(0)
            last_hi(0)
            gate_in(0)
            wqk_in(range(4))
            squares(0)
            wqk_in(range(4, 8))
            scale_shift(lnT, HATA, lnq_gb, pe_hatT, 0, a_lnT)
            act.wait_ge(flag_in, 16)
            act.wait_ge(v_slow, 1)
            with act.Fori(0, BLOCKS - 1) as i:
                attention(i)
                context_in(i + 1, 1)
                for k in range(H // 4):
                    values_in(i, k)
                context_in(i + 1, 3)
                for p in range(PAIRS):
                    exp0(i + 1, p)
                probs0_in(i + 1)
                scale_shift(ffT, HATD, lnf_gb, pe_hatdT, i, a_ffT)
                last_hi(i + 1)
                hidden_in(i, 0)
                hidden_in(i, 1)
                gate_in(i + 1)
                hidden_in(i, 2)
                hidden_in(i, 3)
                squares(i + 1)
                scale_shift(lnT, HATA, lnq_gb, pe_hatT, i + 1, a_lnT)
            attention(BLOCKS - 1)
            for k in range(H // 4):
                values_in(BLOCKS - 1, k)
            scale_shift(ffT, HATD, lnf_gb, pe_hatdT, BLOCKS - 1, a_ffT)
            for k in range(FT // 2):
                hidden_in(BLOCKS - 1, k)

        @block.vector
        def _(dve):
            dve.wait_ge(mrow_in, 16)
            nc.vector.tensor_reduce(any_f[:, :], mask_rows.rearrange("b (c n) -> b c n", c=NCH), AX.X,
                                    ALU.max).then_inc(v_step, 1)
            dve.wait_ge(v_step, 1)
            nc.vector.tensor_reduce(none_f[:, :], any_f[:, :], AX.X, ALU.max).then_inc(v_step, 1)
            dve.wait_ge(v_step, 2)
            nc.vector.tensor_scalar(none_f[:, :], none_f[:, :], -1.0, 1.0, ALU.mult, ALU.add).then_inc(v_step, 1)
            dve.wait_ge(v_step, 3)
            nc.vector.tensor_scalar(flags[:, :], any_f[:, :], none_f[:, 0:1], None, ALU.max).then_inc(v_flag, 1)

            dve.wait_ge(pe_w, 1)
            nc.vector.tensor_copy(wgx[:, :, :], ps[:, 6, :].rearrange("p (t n) -> p t n", t=DT)).then_inc(v_w, 1)
            dve.wait_ge(pe_w, 2)
            nc.vector.tensor_copy(wgcT[:, :, :], ps[:, 7, :].rearrange("p (t n) -> p t n", t=DT)).then_inc(v_w, 1)
            dve.wait_ge(pe_w, 3)
            nc.vector.tensor_scalar(wmz[:, 0, :], ps[:, 5, 0:D], 0.5, None, ALU.mult).then_inc(v_w, 1)
            dve.wait_ge(pe_w, 4)
            nc.vector.tensor_copy(wmz[:, 1, :], ps[:, 4, 0:D]).then_inc(v_w, 1)

            def add_mask(u, c, first=0):
                r, b = u % RING, u // UPB
                return [lambda gg=gg: nc.vector.tensor_tensor_reduce(
                    out=scores[0:G, r, gg, c * CH:(c + 1) * CH], in0=ps[0:G, gg, first:first + CH],
                    in1=mbias[:, b % 2, c * CH:(c + 1) * CH], scale=-1.0, scalar=-NEG,
                    op0=ALU.add, op1=ALU.min, accum_out=cmin[:, r, gg, c:c + 1]) for gg in range(2)]

            def scale_probs(u, c):
                r = u % RING
                for gg in range(2):
                    v = scores[0:G, r, gg, c * CH:(c + 1) * CH]
                    ins = nc.vector.tensor_scalar(v, v, rsum[:, r, gg:gg + 1], None, ALU.mult)
                return ins

            def scores_in(u, i, live):
                r, b = u % RING, u // UPB
                if u % UPB == 0:
                    live[b] = chunk_flags(nc.vector, i, b)
                    wait_apart(dve, p_mask, NB * i + b + 1)
                n, m = PS * (UNITS * i + u), VS * (UNITS * i + u)
                for c in range(NCH):
                    with dve.If(live[b][c] != 0):
                        for gg, add in enumerate(add_mask(u, c)):
                            wait_apart(dve, pe_s, n + 2 * c + gg + 1)
                            add().then_inc(v_s, 1)
                    with dve.Else():
                        nc.vector.memset(cmin[:, r, :, c:c + 1], -NEG).then_inc(v_s, 2)
                nc.vector.memset(sums[:, r, :, :], 0.0).then_inc(v_s, 1)
                dve.wait_ge(v_s, m + VS - 1)
                nc.vector.tensor_reduce(nmax[:, r, :], cmin[:, r, :, :], AX.X, ALU.min).then_inc(v_s, 1)

            def normalise(u, i, live):
                r, b = u % RING, u // UPB
                n = NCH * (UNITS * i + u)
                dve.wait_ge(a_exp, n + NCH)
                nc.vector.tensor_reduce(tsum[:, r, :], sums[:, r, :, :], AX.X, ALU.add).then_inc(v_rs, 1)
                dve.wait_ge(v_rs, 2 * (UNITS * i + u) + 1)
                nc.vector.reciprocal(rsum[:, r, :], tsum[:, r, :]).then_inc(v_rs, 1)
                wait_apart(dve, v_rs, 2 * (UNITS * i + u) + 2)
                for c in range(NCH):
                    with dve.If(live[b][c] != 0):
                        scale_probs(u, c).then_inc(v_prob, 1)
                    with dve.Else():
                        if u or c:
                            dve.wait_ge(v_prob, n + c)
                        dve.sem_inc(v_prob, 1)

            def attention_all(i):
                live = {}
                scores_in(0, i, live)
                scores_in(1, i, live)
                normalise(0, i, live)
                queries_in(i, range(4, 8))
                for u in range(UNITS):
                    if u + 1 < UNITS:
                        normalise(u + 1, i, live)
                    if u + 2 < UNITS:
                        scores_in(u + 2, i, live)

            def scores_last(u, i):
                if u % UPB == 0:
                    dve.wait_ge(p_mask, NB * i + u // UPB + 1)
                for gg, add in enumerate(add_mask(u, NCH - 1, first=ODD)):
                    wait_apart(dve, pe_s, PS * (UNITS * i + u) + PS // 2 * (gg + 1))
                    add().then_inc(v_s, VS // 2)

            def normalise_last(u, i):
                r = u % RING
                dve.wait_ge(a_exp, NCH * (UNITS * i + u + 1))
                nc.vector.reciprocal(rsum[:, r, :], sums[:, r, :, NCH - 1]).then_inc(v_rs, 2)
                dve.wait_ge(v_rs, 2 * (UNITS * i + u + 1))
                scale_probs(u, NCH - 1).then_inc(v_prob, NCH)

            def attention_last(i):
                scores_last(0, i)
                scores_last(1, i)
                normalise_last(0, i)
                queries_in(i, (4,))
                normalise_last(1, i)
                queries_in(i, range(5, 8))
                scores_last(2, i)
                for u in range(UNITS):
                    if u + 3 < UNITS:
                        scores_last(u + 3, i)
                    if u + 2 < UNITS:
                        normalise_last(u + 2, i)

            def attention(i):
                slow = is_slow(nc.vector, i)
                queries_in(i, range(4))
                with dve.If(slow != 0):
                    attention_all(i)
                with dve.Else():
                    attention_last(i)

            def context_in(i, j):
                dve.wait_ge(pe_ctxT, NB * i + j + 1)
                nc.vector.tensor_copy(ctxT[:, j, :].rearrange("p (a n) -> p a n", a=3),
                                      ps[:, SET[0]:SET[0] + 3, 0:500]).then_inc(v_ctxT, 1)

            def queries0(i):
                dve.wait_ge(pe_xT, i + 1)
                nc.vector.tensor_copy(xT[:, :, :].rearrange("p t n -> p (t n)"), ps[:, XTB, :]).then_inc(v_xT, 1)
                dve.wait_ge(pe_q0, i + 1)
                nc.vector.tensor_scalar(q0T[:, :], ps[:, Q0B, 0:TP], float(D) ** -0.5, None,
                                        ALU.mult).then_inc(v_q0, 1)
                dve.wait_ge(pe_zx, i + 1)
                for p in range(PAIRS):
                    nc.vector.tensor_tensor(ya[:, p, :], ps[:, ZXB, p * D:(p + 1) * D], bgate_bc[:, :],
                                            ALU.add).then_inc(v_zx, 1)

            def moments(src, st, p, own, n, done):
                nc.vector.bn_stats(bst[st][:, p, :], src[:, p, :]).then_inc(own, 1)
                wait_apart(dve, own, n)
                nc.vector.bn_aggr(mv[st][:, p, :], bst[st][:, p, :]).then_inc(done, 1)

            def hat(dst, src, st, p, done):
                nc.vector.tensor_scalar(dst[:, p, :], src[:, p, :], mv[st][:, p, 0:1], rstd[st][:, p:p + 1],
                                        ALU.subtract, ALU.mult).then_inc(done, 1)

            def scale_shift(dst, banks, gb, done):
                nc.vector.tensor_scalar(dst[:, 0, :], ps[:, banks[0], 0:TP], gb[:, 0, 0:1], gb[:, 1, 0:1],
                                        ALU.mult, ALU.add).then_inc(done, 1)

            def maxima0(i):
                for p in range(PAIRS):
                    dve.wait_ge(pe_s0, PAIRS * i + p + 1)
                    nc.vector.tensor_reduce(nmax0[:, p:p + 1], ps[:, SET[p]:SET[p] + 3, 0:500], AX.XY, ALU.max,
                                            negate=True).then_inc(v_max0, 1)

            def probs0_in(i):
                dve.wait_ge(pe_p0T, PAIRS * i + 1)
                nc.vector.tensor_copy(p0T[0:KP, 0, :],
                                      ps[0:KP, SET[0]:SET[0] + 3, :].rearrange("p a n -> p (a n)")).then_inc(v_p0T, 1)

            def sums0(i):
                dve.wait_ge(a_p0, PAIRS * i + PAIRS)
                nc.vector.reciprocal(rsum0[:, :], sum0[:, :]).then_inc(v_rs0, 1)

            def contexts0(i, p):
                dve.wait_ge(v_rs0, i + 1)
                dve.wait_ge(pe_c0, PAIRS * i + p + 1)
                nc.vector.tensor_scalar(yb[:, p, 0:E], ps[:, C0B[p], 0:E], rsum0[:, p:p + 1], None,
                                        ALU.mult).then_inc(v_c0, 1)

            def contexts0_T(i):
                dve.wait_ge(pe_c0T, i + 1)
                nc.vector.tensor_copy(c0T[:, :], ps[:, C0TB, 0:TP]).then_inc(v_c0T, 1)

            def last_lo(i):
                dve.wait_ge(a_cT, i + 1)
                nc.vector.tensor_tensor(cT_lo, ctxT[:, :, LAST - ODD:M], cT_hi.bitcast(fp32),
                                        ALU.subtract).then_inc(v_cT, 1)

            def gate(i):
                for p in range(PAIRS):
                    dve.wait_ge(pe_mz, PAIRS * i + p + 1)
                    nc.vector.tensor_tensor(ya[:, p, :], ps[:, MZB[p], D:2 * D], ya[:, p, :], ALU.add).then_inc(v_z, 1)
                for p in range(PAIRS):
                    dve.wait_ge(a_z, PAIRS * i + p + 1)
                    nc.vector.scalar_tensor_tensor(out=yb[:, p, :], in0=yb[:, p, :], scalar=1.0,
                                                   in1=ps[:, MZB[p], 0:D], op0=ALU.add, op1=ALU.mult).then_inc(v_t1, 1)
                    dve.wait_ge(v_t1, PAIRS * i + p + 1)
                    nc.vector.tensor_tensor(yb[:, p, :], yb[:, p, :], xn[:, p, :], ALU.add).then_inc(v_fused, 1)

            def norms(i):
                for p in range(PAIRS):
                    dve.wait_ge(p_rms, PAIRS * i + p + 1)
                    nc.vector.scalar_tensor_tensor(out=x1[:, p, :], in0=yb[:, p, :], scalar=rstd[0][:, p:p + 1],
                                                   in1=normw_bc[:, :], op0=ALU.mult, op1=ALU.mult).then_inc(v_x1, 1)
                    dve.wait_ge(v_x1, PAIRS * i + p + 1)
                    moments(x1, 0, p, v_bns, PAIRS * i + p + 1, v_stat)

            def front_hats(i):
                for p in range(PAIRS):
                    dve.wait_ge(v_stat, PAIRS * i + p + 1)
                    dve.wait_ge(p_stat, PAIRS * i + p + 1)
                    hat(yb, x1, 0, p, v_hat)

            def queries_in(i, pairs):
                for hp in pairs:
                    dve.wait_ge(a_q, 8 * i + hp + 1)
                    nc.vector.tensor_tensor(
                        q_lo[:, :, hp, :, :].rearrange("p b s h -> p h b s"),
                        ps[:, QB[hp], 0:2 * T4].rearrange("p (h b s) -> p h b s", h=2, s=S),
                        q_hi[:, hp, :, 0:S, :].rearrange("p b s h -> p h b s").bitcast(fp32), ALU.subtract).then_inc(v_q, 1)

            def rows_in(i):
                dve.wait_ge(pe_hatT, i + 1)
                scale_shift(lnT, HATA, lnq_gb, v_lnT)

            def tail_in(i, p):
                dve.wait_ge(pe_att, PAIRS * i + p + 1)
                nc.vector.tensor_tensor(x2[:, p, :], ps[:, ATT[p], 0:D], x1[:, p, :], ALU.add).then_inc(v_x2, 1)
                dve.wait_ge(v_x2, PAIRS * i + p + 1)
                moments(x2, 1, p, v_bnsd, PAIRS * i + p + 1, v_statd)

            def tail_hat(i, p):
                dve.wait_ge(out_st, 16 * NB * i + 16)
                dve.wait_ge(v_statd, PAIRS * i + p + 1)
                dve.wait_ge(p_statd, PAIRS * i + p + 1)
                hat(yd, x2, 1, p, v_hatd)

            def tail_rows(i):
                dve.wait_ge(pe_hatdT, i + 1)
                scale_shift(ffT, HATD, lnf_gb, v_ffT)

            def tail_out(i, p):
                dve.wait_ge(pe_y, PAIRS * i + p + 1)
                nc.vector.tensor_tensor(yd[:, p, :], ps[:, YB[p], 0:D], x2[:, p, :], ALU.add).then_inc(v_out, 1)

            dve.sem_inc(v_out, PAIRS)
            dve.wait_ge(bgate_in, 16)
            queries0(0)
            context_in(0, 0)
            context_in(0, 2)
            maxima0(0)
            probs0_in(0)
            sums0(0)
            dve.wait_ge(wo_in, 16)
            dve.wait_ge(a_gate, 1)
            nc.vector.tensor_scalar(wo_sb[:, :, :], wo_sb[:, :, :], gates[:, 2:3], None, ALU.mult).then_inc(v_gated, 1)
            dve.wait_ge(w2_in, 16)
            nc.vector.tensor_scalar(w2_sb[:, :, :], w2_sb[:, :, :], gates[:, 3:4], None, ALU.mult).then_inc(v_gated, 1)
            contexts0(0, 0)
            contexts0(0, 1)
            contexts0_T(0)
            dve.wait_ge(flag_in, 16)
            nc.vector.tensor_reduce(slow_row[:, :], flag_row[0:1, :].rearrange(
                "o (i b c) -> o i b c", b=NB, c=NCH)[:, :, :, 0:NCH - 1], AX.XY, ALU.max).then_inc(v_slow, 1)
            dve.wait_ge(vec_in, 16 * 7)
            last_lo(0)
            gate(0)
            norms(0)
            front_hats(0)
            rows_in(0)
            with dve.Fori(0, BLOCKS - 1) as i:
                attention(i)
                queries0(i + 1)
                context_in(i + 1, 0)
                context_in(i + 1, 2)
                tail_in(i, 0)
                tail_hat(i, 0)
                maxima0(i + 1)
                probs0_in(i + 1)
                tail_in(i, 1)
                sums0(i + 1)
                tail_hat(i, 1)
                contexts0(i + 1, 0)
                tail_rows(i)
                contexts0(i + 1, 1)
                contexts0_T(i + 1)
                last_lo(i + 1)
                gate(i + 1)
                norms(i + 1)
                tail_out(i, 0)
                front_hats(i + 1)
                rows_in(i + 1)
                tail_out(i, 1)
            attention(BLOCKS - 1)
            for p in range(PAIRS):
                tail_in(BLOCKS - 1, p)
            for p in range(PAIRS):
                tail_hat(BLOCKS - 1, p)
            tail_rows(BLOCKS - 1)
            for p in range(PAIRS):
                tail_out(BLOCKS - 1, p)

        @block.tensor
        def _(pe):
            mm, tr = nc.tensor.matmul, nc.tensor.transpose
            pe.wait_ge(p_const, 1)
            pe.wait_ge(wgate_in, 16)
            for half in range(2):
                for f in range(DT):
                    for o in range(DT):
                        c = DT * half + f
                        ins = tr(ps[:, 6 + half, f * D + o * 128:f * D + (o + 1) * 128],
                                 wgate_n[:, o, c * 128:(c + 1) * 128], ident[:, :])
                ins.then_inc(pe_w, 1)
            pe.wait_ge(wmem_in, 16)
            for t in range(DT):
                ins = tr(ps[:, 5, t * 128:(t + 1) * 128], wmem[:, t, :], ident[:, :])
            ins.then_inc(pe_w, 1)
            pe.wait_ge(v_w, 2)
            for t in range(DT):
                ins = mm(ps[:, 4, 0:D], wmem[:, t, :], wgcT[:, t, :], start=(t == 0), stop=(t == DT - 1))
            ins.then_inc(pe_w, 1)

            def transpose_weights(steps):
                for n in steps:
                    if n >= 2:
                        pe.wait_ge(a_w, T_STEP[n - 2])
                    for j in range(4):
                        if n < 4:
                            c = 4 * (n % 2) + j
                            src = wq_n[:, n // 2, c * 128:(c + 1) * 128]
                        else:
                            c = 4 * (n - 4) + j
                            src = wk_n[:, c * 128:(c + 1) * 128]
                        ins = tr(ps[:, n % 2, j * 128:(j + 1) * 128], src, ident[:, :])
                    ins.then_inc(pe_w, 1)

            def key_weights(steps):
                for m in steps:
                    if m >= 2:
                        pe.wait_ge(a_w, K_STEP[m - 2])
                    k, par = m // 2, m % 2
                    rows = slice(64 * par, 64 * par + 64)
                    for t in range(DT):
                        for z in range(2):
                            j, c0 = 2 * k + z, (2 * t + z) * E
                            ins = mm(ps[:, 2 + m % 2, c0:c0 + E], wqT[rows, j, t * 128:(t + 1) * 128],
                                     wkT[rows, j, :], start=True, stop=True)
                    ins.then_inc(pe_w, 1)

            def query_parts(u, gg):
                b, hp = u // UPB, 2 * (u % UPB) + gg
                return [q.rearrange("p s h -> p (s h)") for q in (q_hi[:, hp, b, 0:S, :], q_lo[:, b, hp, :, :])]

            def score_matmul(u, c, gg):
                keys = ctxT[:, u // UPB, c * CH:(c + 1) * CH]
                hi, lo = [q.bitcast(fp32) for q in query_parts(u, gg)]
                mm(ps[0:G, gg, 0:CH], hi, keys, start=True, stop=False)
                return mm(ps[0:G, gg, 0:CH], lo, keys, start=False, stop=True)

            def last_score_matmul(u, gg):
                hi, lo = query_parts(u, gg)
                keys_hi, keys_lo = cT_hi[:, u // UPB, :], cT_lo[:, u // UPB, :]
                mm(ps[0:G, gg, 0:CH + ODD], hi, keys_hi, start=True, stop=False)
                mm(ps[0:G, gg, 0:CH + ODD], hi, keys_lo, start=False, stop=False)
                return mm(ps[0:G, gg, 0:CH + ODD], lo, keys_hi, start=False, stop=True)

            def transpose_probs(u, c):
                r, slot = u % RING, (u + c) % 2
                for t in range(KT):
                    for gg in range(2):
                        col = (t % 2) * 256 + gg * G
                        ins = tr(ps[0:KP, 2 + 2 * slot + t // 2, col:col + G],
                                 scores[0:G, r, gg, c * CH + t * KP:c * CH + (t + 1) * KP], ident[0:G, 0:G])
                return ins

            def unit_scores(u, i, live):
                b = u // UPB
                n, m = PS * (UNITS * i + u), VS * (UNITS * i + u)
                if u % UPB == 0:
                    live[b] = chunk_flags(nc.tensor, i, b)
                for c in range(NCH):
                    with pe.If(live[b][c] != 0):
                        for gg in range(2):
                            if c:
                                pe.wait_ge(v_s, m + 2 * c - 1 + gg)
                            elif u:
                                pe.wait_ge(v_s, m)
                            score_matmul(u, c, gg).then_inc(pe_s, 1)
                    with pe.Else():
                        if u or c:
                            pe.wait_ge(pe_s, n + 2 * c)
                        pe.sem_inc(pe_s, 2)

            def unit_pT(u, i, live):
                b = u // UPB
                n = NCH * (UNITS * i + u)
                for c in range(NCH):
                    with pe.If(live[b][c] != 0):
                        pe.wait_ge(v_prob, n + c + 1)
                        if c == 1 and u:
                            pe.wait_ge(a_pT, n - 1)
                        elif c != 1 and (u or c):
                            pe.wait_ge(a_pT, n + max(c - 1, 0))
                        transpose_probs(u, c).then_inc(pe_pT, 1)
                    with pe.Else():
                        if u or c:
                            pe.wait_ge(pe_pT, n + c)
                        pe.sem_inc(pe_pT, 1)
                    if c < NCH - 1:
                        unit_pv(u, c, i, live)

            def unit_pv(u, c, i, live):
                b, slot = u // UPB, (u + c) % 2
                if c == 0:
                    if u >= 2:
                        pe.wait_ge(a_o, UNITS * i + u - 1)
                    mm(ps[:, 6 + u % 2, 0:U], zeros[0:1, :], any_row(b), start=True, stop=False,
                       skip_group_check=True)
                with pe.If(live[b][c] != 0):
                    pe.wait_ge(a_pT, NCH * (UNITS * i + u) + c + 1)
                    for t in range(KT):
                        mm(ps[:, 6 + u % 2, 0:U], ctx[:, b, KT * c + t, :], pT[:, slot, t, :],
                           start=False, stop=False, skip_group_check=True)

            def any_row(b):
                return ctx[0:1, b, 0:2, :].rearrange("p t e -> p (t e)")[:, 0:U]

            def attention_all(i, more):
                live = {}
                pe.wait_ge(v_q, 8 * i + 4)
                unit_scores(0, i, live)
                unit_scores(1, i, live)
                queries1(i, range(4, 8))
                pe.wait_ge(v_q, 8 * i + 8)
                for u in range(UNITS):
                    unit_pT(u, i, live)
                    if u + 2 < UNITS:
                        unit_scores(u + 2, i, live)
                    elif more:
                        next_rows(i, u + 2 - UNITS)
                    unit_pv(u, NCH - 1, i, live)
                    mm(ps[:, 6 + u % 2, 0:U], zeros[0:1, :], any_row(u // UPB), start=False, stop=True,
                       skip_group_check=True).then_inc(pe_o, 1)

            def last_scores(u, i):
                for gg in range(2):
                    if u:
                        pe.wait_ge(v_s, VS * (UNITS * i + u - 1) + VS // 2 * (gg + 1))
                    last_score_matmul(u, gg).then_inc(pe_s, PS // 2)

            def last_pT(u, i):
                pe.wait_ge(v_prob, NCH * (UNITS * i + u + 1))
                if u >= 2:
                    pe.wait_ge(a_pT, NCH * (UNITS * i + u - 1))
                transpose_probs(u, NCH - 1).then_inc(pe_pT, NCH)

            def last_pv(u, i):
                b, slot = u // UPB, (u + NCH - 1) % 2
                pe.wait_ge(a_pT, NCH * (UNITS * i + u + 1))
                if u >= 2:
                    pe.wait_ge(a_o, UNITS * i + u - 1)
                for t in range(KT):
                    ins = mm(ps[:, 6 + u % 2, 0:U], ctx[:, b, KT * (NCH - 1) + t, :], pT[:, slot, t, :],
                             start=(t == 0), stop=(t == KT - 1))
                ins.then_inc(pe_o, 1)

            def attention_last(i, more):
                pe.wait_ge(v_q, 8 * i + 2)
                last_scores(0, i)
                queries1(i, (4,))
                pe.wait_ge(v_q, 8 * i + 4)
                last_scores(1, i)
                queries1(i, range(5, 8))
                last_pT(0, i)
                pe.wait_ge(v_q, 8 * i + 6)
                last_scores(2, i)
                last_pT(1, i)
                pe.wait_ge(v_q, 8 * i + 8)
                for u in range(UNITS):
                    if u + 3 < UNITS:
                        last_scores(u + 3, i)
                    elif more and u != UNITS - 2:
                        next_rows(i, u // (UNITS - 1))
                    if 1 < u + 1 < UNITS:
                        last_pT(u + 1, i)
                    last_pv(u, i)

            def next_rows(i, part):
                if part == 0:
                    pe.wait_ge(v_s, VS * (UNITS * i + UNITS))
                    rows0(i + 1)
                else:
                    queries0(i + 1)

            def attention(i, more=True):
                slow = is_slow(nc.tensor, i)
                pe.wait_ge(v_lnT, i + 1)
                pe.wait_ge(a_lnT, i + 1)
                queries1(i, range(4))
                pe.wait_ge(v_cT, i + 1)
                pe.wait_ge(v_out, PAIRS * (i + 1))
                with pe.If(slow != 0):
                    attention_all(i, more)
                with pe.Else():
                    attention_last(i, more)

            def context_T(i, j):
                pe.wait_ge(ctx_in_s[j], 16 * i + 16)
                if j >= 2:
                    pe.wait_ge((v_ctxT, a_ctxT)[j % 2], 2 * i + 1)
                for t in range(NT):
                    ins = tr(ps[:, SET[j % 2] + t // 4, (t % 4) * KP:(t % 4 + 1) * KP], ctx[:, j, t, :],
                             ident[0:KP, 0:KP])
                ins.then_inc(pe_ctxT, 1)

            def row_transposes(banks, src):
                for t in range(DT):
                    for p in range(PAIRS):
                        col = (t // len(banks)) * TP + p * 128
                        ins = tr(ps[:, banks[t % len(banks)], col:col + 128],
                                 src[:, p, t * 128:(t + 1) * 128], ident[:, :])
                return ins

            def rows0(i):
                pe.wait_ge(x_in, 16 * NB * i + 16 * NB)
                row_transposes((XTB,), xn).then_inc(pe_xT, 1)

            def queries0(i):
                pe.wait_ge(v_xT, i + 1)
                for t in range(DT):
                    ins = mm(ps[:, Q0B, 0:TP], wmem[:, t, :], xT[:, t, :], start=(t == 0), stop=(t == DT - 1))
                ins.then_inc(pe_q0, 1)
                for p in range(PAIRS):
                    for t in range(DT):
                        ins = mm(ps[:, ZXB, p * D:(p + 1) * D], xT[:, t, p * 128:(p + 1) * 128], wgx[:, t, :],
                                 start=(t == 0), stop=(t == DT - 1))
                ins.then_inc(pe_zx, 1)

            def scores0(i):
                pe.wait_ge(v_q0, i + 1)
                pe.wait_ge(v_ctxT, 2 * i + 2)
                for p in range(PAIRS):
                    pe.wait_ge(a_ctxT, 2 * i + 1 + p)
                    for k in range(3):
                        for hb in range(2):
                            j = 2 * p + hb
                            ins = mm(ps[SP * hb:SP * hb + SP, SET[p] + k, 0:500], q0T[:, j * SP:(j + 1) * SP],
                                     ctxT[:, j, k * 500:(k + 1) * 500], start=True, stop=True)
                    ins.then_inc(pe_s0, 1)

            def probs0_T(i, p):
                pe.wait_ge(a_p0, PAIRS * i + p + 1)
                for t in range(NT):
                    ins = tr(ps[0:KP, SET[p] + t // 4, (t % 4) * 128:(t % 4 + 1) * 128],
                             p0[:, p, t * KP:(t + 1) * KP], ident[:, :])
                ins.then_inc(pe_p0T, 1)

            def contexts0(i, p):
                pe.wait_ge(v_p0T if p == 0 else a_p0T, i + 1)
                for t in range(NT):
                    for hb in range(2):
                        ins = mm(ps[SP * hb:SP * hb + SP, C0B[p], 0:E],
                                 p0T[0:KP, p, t * 128 + hb * SP:t * 128 + hb * SP + SP], ctx[:, 2 * p + hb, t, :],
                                 start=(t == 0), stop=(t == NT - 1))
                ins.then_inc(pe_c0, 1)

            def contexts0_T(i):
                for p in range(PAIRS):
                    pe.wait_ge(v_c0, PAIRS * i + p + 1)
                    ins = tr(ps[:, C0TB, p * 128:(p + 1) * 128], yb[:, p, 0:E], ident[:, :])
                ins.then_inc(pe_c0T, 1)

            def projections0(i):
                pe.wait_ge(v_c0T, i + 1)
                for p in range(PAIRS):
                    mm(ps[:, MZB[p], :], c0T[:, p * 128:(p + 1) * 128],
                       wmz[:, :, :].rearrange("p a n -> p (a n)"), start=True, stop=True).then_inc(pe_mz, 1)

            def unpadded(rows):
                return [rows[:, t, :].rearrange("p (b s) -> p b s", s=SP)[:, :, 0:S] for t in range(DT)]

            def rows1(i):
                pe.wait_ge(v_hat, PAIRS * i + PAIRS)
                row_transposes(HATA, yb).then_inc(pe_hatT, 1)

            def queries1(i, pairs):
                tok = unpadded(lnT)
                for hp in pairs:
                    for h in range(2):
                        for t in range(DT):
                            ins = mm(ps[:, QB[hp], h * T4:(h + 1) * T4], wqk[:, t, 2 * hp + h, :], tok[t],
                                     start=(t == 0), stop=(t == DT - 1))
                    ins.then_inc(pe_q, 1)

            def values(i, k):
                for z in range(2):
                    j = 2 * k + z
                    for hb in range(2):
                        ins = mm(ps[DH * hb:DH * hb + DH, VB[k], z * T4:(z + 1) * T4], wv_sb[:, 2 * j + hb, :],
                                 oT[:, j, :, 0:S, hb], start=True, stop=True)
                ins.then_inc(pe_v, 1)

            def attention_out(i, p, tiles):
                for j in tiles:
                    ins = mm(ps[:, ATT[p], 0:D], vT[:, j, 2 * p:2 * p + 2, :].rearrange("p b s -> p (b s)"),
                             wo_sb[:, j, :], start=(j == 0), stop=(j == H // 2 - 1))
                return ins

            def rows_ff(i):
                pe.wait_ge(v_hatd, PAIRS * i + PAIRS)
                row_transposes(HATD, yd).then_inc(pe_hatdT, 1)

            def hidden(i, k):
                pe.wait_ge(w1_in, 16)
                pe.wait_ge(v_ffT, i + 1)
                pe.wait_ge(a_ffT, i + 1)
                tok = unpadded(ffT)
                for f in range(2):
                    ft = 2 * k + f
                    for t in range(DT):
                        ins = mm(ps[:, W1B[k], f * T4:(f + 1) * T4], w1_sb[:, t, ft * 128:(ft + 1) * 128],
                                 tok[t], start=(t == 0), stop=(t == DT - 1))
                ins.then_inc(pe_h, 1)

            def feed_forward_out(i, p, tiles):
                for f in tiles:
                    if p == 0 and f % 2 == 0:
                        pe.wait_ge(a_gelu, 4 * i + f // 2 + 1)
                    ins = mm(ps[:, YB[p], 0:D], h1T[:, f, 2 * p:2 * p + 2, :].rearrange("p b s -> p (b s)"),
                             w2_sb[:, f, :], start=(f == 0), stop=(f == FT - 1))
                return ins

            rows0(0)
            queries0(0)
            pe.wait_ge(v_w, 4)
            context_T(0, 0)
            context_T(0, 1)
            pe.wait_ge(wq_in, 16)
            pe.wait_ge(v_zx, PAIRS)
            transpose_weights(range(4))
            context_T(0, 2)
            context_T(0, 3)
            pe.wait_ge(wk_in, 16)
            transpose_weights(range(4, 6))
            scores0(0)
            probs0_T(0, 0)
            probs0_T(0, 1)
            pe.wait_ge(a_w, T_STEP[5])
            for p in range(PAIRS):
                contexts0(0, p)
            contexts0_T(0)
            projections0(0)
            key_weights(range(8))
            rows1(0)
            pe.wait_ge(a_w, K_STEP[7])
            pe.wait_ge(flag_in, 16)
            pe.wait_ge(v_slow, 1)
            with pe.Fori(0, BLOCKS - 1) as i:
                attention(i)
                context_T(i + 1, 0)
                pe.wait_ge(a_o, UNITS * i + UNITS)
                context_T(i + 1, 1)
                pe.wait_ge(wv_in, 16)
                pe.wait_ge(v_zx, PAIRS * (i + 1) + PAIRS)
                values(i, 0)
                values(i, 1)
                context_T(i + 1, 2)
                for k in (2, 3):
                    pe.wait_ge(a_v, 4 * i + k - 1)
                    values(i, k)
                context_T(i + 1, 3)
                pe.wait_ge(a_v, 4 * i + 4)
                pe.wait_ge(p_pad, i + 1)
                pe.wait_ge(v_gated, 1)
                attention_out(i, 0, range(H // 2)).then_inc(pe_att, 1)
                scores0(i + 1)
                attention_out(i, 1, range(H // 4))
                probs0_T(i + 1, 0)
                attention_out(i, 1, range(H // 4, H // 2)).then_inc(pe_att, 1)
                probs0_T(i + 1, 1)
                pe.wait_ge(v_x2, PAIRS * i + PAIRS)
                contexts0(i + 1, 0)
                pe.wait_ge(a_p0T, i + 2)
                rows_ff(i)
                contexts0(i + 1, 1)
                hidden(i, 0)
                contexts0_T(i + 1)
                hidden(i, 1)
                projections0(i + 1)
                hidden(i, 2)
                hidden(i, 3)
                pe.wait_ge(v_gated, 2)
                feed_forward_out(i, 0, range(FT)).then_inc(pe_y, 1)
                feed_forward_out(i, 1, range(FT - 2))
                rows1(i + 1)
                feed_forward_out(i, 1, range(FT - 2, FT)).then_inc(pe_y, 1)
            attention(BLOCKS - 1, more=False)
            pe.wait_ge(a_o, UNITS * BLOCKS)
            for k in range(H // 4):
                if k >= 2:
                    pe.wait_ge(a_v, 4 * (BLOCKS - 1) + k - 1)
                values(BLOCKS - 1, k)
            pe.wait_ge(a_v, 4 * BLOCKS)
            pe.wait_ge(p_pad, BLOCKS)
            for p in range(PAIRS):
                attention_out(BLOCKS - 1, p, range(H // 2)).then_inc(pe_att, 1)
            rows_ff(BLOCKS - 1)
            for k in range(FT // 2):
                hidden(BLOCKS - 1, k)
            for p in range(PAIRS):
                feed_forward_out(BLOCKS - 1, p, range(FT)).then_inc(pe_y, 1)


_INS = ['x', 'ctx_1024', 'mask_BxS2_bk0', 'L0_xattn_W_mem', 'L0_xattn_W_gate', 'L0_xattn_b_gate',
        'L0_xattn_norm_w', 'L1_xattn_ln_q_g', 'L1_xattn_ln_q_b', 'L1_xattn_Wq', 'L1_xattn_Wkv', 'L1_xattn_Wo',
        'L1_xattn_attn_gate', 'L1_xattn_ln_ff_g', 'L1_xattn_ln_ff_b', 'L1_xattn_W1', 'L1_xattn_W2',
        'L1_xattn_ff_gate']


def kernel(**inputs):
    import numpy as _np
    import concourse.bacc as _bacc
    from concourse import mybir as _mybir
    from concourse.bass_utils import run_bass_kernel_spmd as _run

    nc = _bacc.Bacc("TRN2", target_bir_lowering=False, num_devices=1)
    arrays, args = {}, []
    for name in _INS:
        a = _np.ascontiguousarray(inputs[name])
        arrays[f"in_{name}_dram"] = a
        args.append(nc.dram_tensor(f"in_{name}_dram", a.shape, _mybir.dt.from_np(a.dtype), kind="ExternalInput").ap())
    shape = inputs['x'].shape
    args.append(nc.dram_tensor("out_0_dram", shape, _mybir.dt.float32, kind="ExternalOutput").ap())
    xattn_kernel(nc, *args)
    r = _run(nc, [arrays], core_ids=[0])
    return r.results[0]["out_0_dram"]
```
